# Optimizing a Trainium2 kernel written in Bass

```python
import numpy as np
import jax
import jax.numpy as jnp

def _softmax(x, axis=-1):
    return jax.nn.softmax(x, axis=axis)

def _gelu(x):
    return jax.nn.gelu(x, approximate=True)

def _silu(x):
    return jax.nn.silu(x)

def _sigmoid(x):
    return jax.nn.sigmoid(x)

def _layernorm(x, axis=-1, eps=1e-05):
    m = jnp.mean(x, axis=axis, keepdims=True)
    v = jnp.var(x, axis=axis, keepdims=True)
    return (x - m) / jnp.sqrt(v + eps)

def _scatter_add(tgt, idx, src, axis=0):
    return tgt.at[idx].add(src)

def _segment_sum(src, seg, n):
    return jax.ops.segment_sum(src, seg, n)
kernel_name = 'mk_seq_preln_d1_jaxref_r4_c6da50'

def setup_inputs(seed: int=0):
    np.random.seed(seed)
    _w = jnp.asarray

    def _L0_attn_setup():
        import jax, jax.numpy as jnp
        import numpy as np
        B, T, D = (4, 1024, 256)
        HD = 64
        H = D // HD
        C = 64
        key = jax.random.key(seed)
        k1, k2, k3 = jax.random.split(key, 3)
        out = jax.random.normal(k1, (B, T, D), jnp.float32)
        W_write = jax.random.normal(k2, (D, D), jnp.float32) * 0.03
        W_read = jax.random.normal(k3, (D, D), jnp.float32) * 0.03
        decay = jnp.full((H,), 4.6, jnp.float32)
        log_alpha = jnp.log(jnp.full((H,), 0.03, jnp.float32))
        return {'out': out, 'W_write': W_write, 'W_read': W_read, 'decay': decay, 'log_alpha': log_alpha}
    _L0_attn_in = _L0_attn_setup()

    def _L0_ffn_setup():
        import jax, jax.numpy as jnp
        import numpy as np
        NUM_EXPERTS = 8
        TOP_K = 2
        key = jax.random.key(seed)
        ks = jax.random.split(key, 6)
        B, S, D, F = (2, 512, 256, 1024)
        E = NUM_EXPERTS
        sd = 1.0 / np.sqrt(D)
        sf = 1.0 / np.sqrt(F)
        return {'x': jax.random.normal(ks[0], (B, S, D), dtype=jnp.float32), 'gate_w': jax.random.normal(ks[1], (E, D), dtype=jnp.float32) * sd, 'w1': jax.random.uniform(ks[2], (F, E, D), dtype=jnp.float32, minval=-sd, maxval=sd), 'b1': jax.random.uniform(ks[3], (E, F), dtype=jnp.float32, minval=-sd, maxval=sd), 'w2': jax.random.uniform(ks[4], (D, E, F), dtype=jnp.float32, minval=-sf, maxval=sf), 'b2': jax.random.uniform(ks[5], (E, D), dtype=jnp.float32, minval=-sf, maxval=sf)}
    _L0_ffn_in = _L0_ffn_setup()
    _d = {'L0_attn_out': _L0_attn_in['out'], 'L0_attn_W_write': _L0_attn_in['W_write'], 'L0_attn_W_read': _L0_attn_in['W_read'], 'L0_attn_decay': _L0_attn_in['decay'], 'L0_attn_log_alpha': _L0_attn_in['log_alpha'], 'L0_ffn_gate_w': _L0_ffn_in['gate_w'], 'L0_ffn_w1': _L0_ffn_in['w1'], 'L0_ffn_b1': _L0_ffn_in['b1'], 'L0_ffn_w2': _L0_ffn_in['w2'], 'L0_ffn_b2': _L0_ffn_in['b2']}
    _x0 = _d['L0_attn_out']
    _d['L0_attn_out'] = jax.random.normal(jax.random.fold_in(jax.random.key(seed), 1), (2, 2048, 256), dtype=_x0.dtype)
    del _x0
    return _d

def reference(L0_attn_out, L0_attn_W_write, L0_attn_W_read, L0_attn_decay, L0_attn_log_alpha, L0_ffn_gate_w, L0_ffn_w1, L0_ffn_b1, L0_ffn_w2, L0_ffn_b2):

    def _L0_attn_ref(out, W_write, W_read, decay, log_alpha):
        import jax, jax.numpy as jnp
        import numpy as np
        B, T, D = (4, 1024, 256)
        HD = 64
        H = D // HD
        C = 64
        Bb, Tt, Dd = out.shape
        d, Hh, Cc = (HD, D // HD, C)
        out32 = out.astype(jnp.float32)
        gamma = jax.nn.sigmoid(decay)
        log_gamma = jnp.log(gamma)
        v = (out32 @ W_write.T).reshape(Bb, Tt, Hh, d).transpose(0, 2, 1, 3)
        rk = out32.reshape(Bb, Tt, Hh, d).transpose(0, 2, 1, 3)
        wk = jnp.pad(rk[:, :, :-1], ((0, 0), (0, 0), (1, 0), (0, 0)))
        BH = Bb * Hh
        gamma_bh = jnp.tile(gamma, Bb)
        log_gamma_bh = jnp.tile(log_gamma, Bb)
        nC = Tt // Cc
        v_ch = v.reshape(BH, nC, Cc, d).transpose(1, 0, 2, 3)
        rk_ch = rk.reshape(BH, nC, Cc, d).transpose(1, 0, 2, 3)
        wk_ch = wk.reshape(BH, nC, Cc, d).transpose(1, 0, 2, 3)
        p = jnp.arange(Cc)
        diffs = jnp.clip(p[:, None] - 1 - p[None, :], 0)
        causal = p[:, None] > p[None, :]
        M = jnp.exp(diffs[None].astype(jnp.float32) * log_gamma_bh[:, None, None]) * causal[None]
        g_p = gamma_bh[:, None] ** p[None, :].astype(jnp.float32)
        g_w = gamma_bh[:, None] ** (Cc - 1 - p)[None, :].astype(jnp.float32)
        g_C = gamma_bh ** Cc

        def scan_fn(W, chunk):
            rk_c, wk_c, v_c = chunk
            inter = jnp.einsum('bij,bcj->bci', W, rk_c) * g_p[:, :, None]
            S = jnp.einsum('bcd,bkd->bck', rk_c, wk_c)
            intra = jnp.einsum('bck,bkd->bcd', S * M, v_c)
            W_new = g_C[:, None, None] * W + jnp.einsum('bci,bcj->bij', v_c * g_w[:, :, None], wk_c)
            return (W_new, inter + intra)
        W0 = jnp.zeros((BH, d, d), jnp.float32)
        _, reads = jax.lax.scan(scan_fn, W0, (rk_ch, wk_ch, v_ch))
        reads = reads.transpose(1, 0, 2, 3).reshape(Bb, Hh, Tt, d)
        alpha = jnp.exp(log_alpha)[None, :, None, None]
        reads = (alpha * reads).transpose(0, 2, 1, 3).reshape(Bb, Tt, Dd)
        return out + (reads @ W_read.T).astype(out.dtype)

    def _L0_ffn_ref(x, gate_w, w1, b1, w2, b2):
        import jax, jax.numpy as jnp
        import numpy as np
        NUM_EXPERTS = 8
        TOP_K = 2
        logits = jnp.einsum('bsd,ed->bse', x, gate_w)
        probs = jax.nn.softmax(logits, axis=-1)
        topk_probs, topk_idx = jax.lax.top_k(probs, TOP_K)
        oh = jax.nn.one_hot(topk_idx, NUM_EXPERTS, dtype=x.dtype)
        h = jnp.einsum('bsd,fed,bske->bskf', x, w1, oh)
        h = h + jnp.take(b1, topk_idx, axis=0)
        h = jax.nn.gelu(h)
        y = jnp.einsum('bskf,def,bske->bskd', h, w2, oh)
        y = y + jnp.take(b2, topk_idx, axis=0)
        out = jnp.sum(y * topk_probs[..., None], axis=-2)
        return out
    x = L0_attn_out
    x = x + _L0_attn_ref(_layernorm(x, axis=-1), L0_attn_W_write, L0_attn_W_read, L0_attn_decay, L0_attn_log_alpha)
    x = x + _L0_ffn_ref(_layernorm(x, axis=-1), L0_ffn_gate_w, L0_ffn_w1, L0_ffn_b1, L0_ffn_w2, L0_ffn_b2)
    return x

_drawn_inputs = setup_inputs


def setup_inputs(seed=0):
    import zlib

    import numpy as np

    out = dict(_drawn_inputs(seed))
    spreads = {'L0_attn_decay': (4.599999904632568, 0.2), 'L0_attn_log_alpha': (-3.5065579414367676, 0.2)}
    factors = {'L0_ffn_b1': 8.0, 'L0_ffn_b2': 8.0}
    for name, (base, spread) in spreads.items():
        noise = np.random.default_rng([zlib.crc32(name.encode()), seed]).standard_normal(out[name].shape)
        drawn = base * np.exp(spread * noise) if base else spread * noise
        out[name] = jnp.asarray(drawn.astype(out[name].dtype))
    for name, factor in factors.items():
        out[name] = (out[name] * factor).astype(out[name].dtype)
    return out
```

```python
from contextlib import ExitStack

import numpy as np

import concourse.bass as bass
from concourse import mybir

F32 = mybir.dt.float32
F16 = mybir.dt.float16
BF16 = mybir.dt.bfloat16
I32 = mybir.dt.int32
U32 = mybir.dt.uint32
ALU = mybir.AluOpType
ACT = mybir.ActivationFunctionType
AX = mybir.AxisListType

P = 128
B, T, D = 2, 2048, 256
H, HD = 4, 64
E, F = 8, 1024
KD = D // P
MF = F // P
NCH = T // P
TOK = B * T
EPS = 1e-5
TILE = 256
CAP = TOK + TILE
NT = (2 * TOK + E * (TILE - 1)) // TILE
ROW = D + E + 1
WSCALE = 64.0
PIECE = 1024
NPIECE = E * 4
EW = 4 * 2 * PIECE
LAG = 5
PEEL1 = LAG + 2

CONST = {}
_at = 0
for _name, _width in (("ident", P), ("before", P), ("gap", P), ("index", P), ("left", 1), ("experts", E),
                      ("region", E), ("token", 2 * NCH), ("padtoken", 2), ("step", TOK // TILE),
                      ("upto", E * E), ("tile", NT)):
    CONST[_name] = (_at, _width)
    _at += _width
NCONST = _at


def constants():
    c = np.zeros((P, NCONST), np.float32)
    p = np.arange(P)[:, None]
    f = np.arange(P)[None, :]

    def put(name, value):
        a, w = CONST[name]
        c[:, a:a + w] = value

    put("ident", p == f)
    put("before", p < f)
    put("gap", np.maximum(f - 1 - p, 0))
    put("index", f)
    put("left", P - 1 - p)
    put("experts", np.arange(E)[None, :])
    put("region", np.arange(E)[None, :] * CAP)
    q = np.arange(2 * NCH)[None, :]
    put("token", (q % 2) * T + (q // 2) * P + p)
    put("padtoken", TOK + 2 * p + np.arange(2)[None, :])
    put("step", np.arange(TOK // TILE)[None, :] * TILE)
    put("upto", (np.arange(E)[None, :] <= np.arange(E)[:, None]).reshape(1, -1))
    put("tile", np.arange(NT)[None, :])
    return c


def build(nc, x, w_write, w_read, decay, log_alpha, gate_w, experts, b1, b2, const, out):
    with ExitStack() as ctx:
        def sb(name, shape, dt=F32):
            return ctx.enter_context(nc.sbuf_tensor(name, shape, dt))

        def sem(name):
            return ctx.enter_context(nc.semaphore(name))

        sent = nc.dram_tensor("sent_rows", (E * CAP + TILE, ROW), F32, kind="Internal").ap()
        x_rows = x.rearrange("b t d -> (b t) d")

        weights = sb("weights", [P, E * EW], F16)
        consts = sb("consts", [P, NCONST])

        def const_of(name, rows=P):
            a, w = CONST[name]
            return consts[0:rows, a:a + w]

        ident = const_of("ident")
        before = const_of("before")
        ident16 = sb("ident16", [P, P], F16)
        before16 = sb("before16", [P, P], BF16)
        ones16 = sb("ones16", [P, P], BF16)
        wwT = sb("wwT", [P, KD, D])
        wrT = sb("wrT", [P, KD, D])
        gateT = sb("gateT", [P, KD, E])
        rates = sb("rates", [P, 6])
        alphas = sb("alphas", [P, 6])
        gam = sb("gam", [P, 6])
        lng = sb("lng", [P, 6])
        decayM = sb("decayM", [P, 2, KD, P])
        decayQ = sb("decayQ", [P, KD, P])
        decayK = sb("decayK", [P, H])
        decayC = sb("decayC", [P, KD])
        b1T = sb("b1T", [P, E, MF])
        minus_half = sb("minus_half", [P, 1])
        zcol = sb("zcol", [P, B * KD, 1])
        base = sb("base", [P, E])
        token_i = sb("token_i", [P, 2 * NCH], I32)
        pad = sb("pad", [P, 2, ROW])
        tab = sb("tab", [1, 3 * E + 6 * NT])
        cmp = sb("cmp", [1, max(E * TOK // TILE, NT * E)])
        tab_i = sb("tab_i", [1, E + 2 * NT], I32)
        pad_row_i = tab_i[:, 0:E]
        tile_row_i = tab_i[:, E:E + NT]
        tile_exp_i = tab_i[:, E + NT:E + 2 * NT]

        ARENA = 16128
        arena = sb("arena", [P, ARENA])
        at = [0]

        def carve(words):
            a = at[0]
            at[0] += words
            assert at[0] <= ARENA, at[0]
            return arena[:, a:a + words]

        res = carve(4 * 2 * D)
        xt = carve(2 * 2 * D).rearrange("p (s b d) -> p s b d", s=2, b=2)
        xn = carve(2 * 2 * D).rearrange("p (s b d) -> p s b d", s=2, b=2)
        xnT = carve(2 * 2 * KD * (P + 1)).rearrange("p (s b k t) -> p s b k t", s=2, b=2, k=KD)
        keys = carve(2 * 2 * D).rearrange("p (s b d) -> p s b d", s=2, b=2)
        queries = carve(2 * D).rearrange("p (b k t) -> p b k t", b=2, k=KD)
        vals = carve(2 * D).rearrange("p (b d) -> p b d", b=2)
        scores = carve(2 * H * P).rearrange("p (b s k t) -> p b s k t", b=2, s=2, k=KD)
        readsT = carve(2 * 2 * KD * (P + 1)).rearrange("p (s b k t) -> p s b k t", s=2, b=2, k=KD)
        xm = carve(2 * 2 * D).rearrange("p (s b d) -> p s b d", s=2, b=2)
        xmT = carve(2 * D).rearrange("p (b k t) -> p b k t", b=2, k=KD)
        row = carve(2 * 2 * ROW).rearrange("p (s b w) -> p s b w", s=2, b=2)
        state = carve(2 * D).rearrange("p (b k i) -> p b k i", b=2, k=KD)
        faded = carve(2 * D).rearrange("p (b k i) -> p b k i", b=2, k=KD)
        staged = carve(2 * PIECE).rearrange("p (b w) -> p b w", b=2)
        end_one = at[0]
        at[0] = 0
        wcur = carve(EW).bitcast(F16).rearrange("p (s w) -> p s w", s=2)
        b2_all = carve(E * D)
        tile_in = carve(2 * 2 * ROW).rearrange("p (s c w) -> p s c w", s=2, c=2)
        tileT = carve(2 * 4 * TILE // 2).bitcast(F16).rearrange("p (s k t) -> p s k t", s=2, k=4)
        act = carve(2 * 2 * TILE).rearrange("p (s w) -> p s w", s=2)
        h_hi = carve(2 * TILE).bitcast(F16).rearrange("p (s m t) -> p s m t", s=2, m=2)
        h_lo = carve(2 * TILE).bitcast(F16).rearrange("p (s m t) -> p s m t", s=2, m=2)
        yout = carve(2 * 2 * D).rearrange("p (s c d) -> p s c d", s=2, c=2)
        b1_cur = carve(2 * MF).rearrange("p (s m) -> p s m", s=2)
        b2_cur = carve(2 * D).rearrange("p (s d) -> p s d", s=2)
        gate_cur = carve(4).rearrange("p (s c) -> p s c", s=2)
        tok_cur = carve(4).bitcast(I32).rearrange("p (s c) -> p s c", s=2)
        zrow = arena[:, end_one:end_one + 2 * D]
        assert end_one + 2 * D <= ARENA

        small_at = [0]
        tiny = sb("tiny", [P, 176])

        def small(w, dt=F32):
            a = small_at[0]
            small_at[0] += w
            v = tiny[:, a:a + w]
            return v if dt == F32 else v.bitcast(dt)

        by_batch = lambda v: v.rearrange("p (b e) -> p b e", b=B)
        stats1 = by_batch(small(B * 6))
        moments1 = by_batch(small(B * 2))
        ve1, rs1 = small(B), small(B)
        stats2 = by_batch(small(B * 6))
        moments2 = by_batch(small(B * 2))
        ve2, rs2 = small(B), small(B)
        logit = by_batch(small(B * E))
        top = by_batch(small(B * 8))
        top_at = by_batch(small(B * 8, U32))
        shifted = by_batch(small(B * E))
        masked = by_batch(small(B * E))
        esum, rsum = small(B), small(B)
        slot_i = small(B * 2, I32)
        slots = by_batch(small(B * E))
        assert small_at[0] <= 176
        pick = sb("pick", [P, B, 2, E])
        picked = sb("picked", [P, B, 2, E])
        mask = sb("mask", [P, B, E], BF16)

        psum = ctx.enter_context(nc.psum_tensor("psum", [P, 8, 512], F32))
        ps_xT = psum[:, 0, :].rearrange("p (b k t) -> p b k t", b=2, k=KD)
        ps_mT = psum[:, 1, :].rearrange("p (b k t) -> p b k t", b=2, k=KD)
        ps_rank = psum[:, 0, 0:B * E].rearrange("p (b e) -> p b e", b=B)
        ps_total = psum[:, 0, B * E:B * E + E]
        ps_logit = psum[:, 1, 0:B * E].rearrange("p (b e) -> p b e", b=B)
        ps_val = psum[:, 2, :].rearrange("p (b d) -> p b d", b=2)
        ps_score = psum[:, 3:5, :].rearrange("p s (b w) -> p s b w", b=2)
        ps_read = psum[:, 5, :].rearrange("p (b k t) -> p b k t", b=2, k=KD)
        ps_state = psum[:, 6, :].rearrange("p (b k i) -> p b k i", b=2, k=KD)
        ps_proj = psum[:, 7, :].rearrange("p (b d) -> p b d", b=2)
        ps_h = psum[:, 0:2, :].rearrange("p s (m t) -> p s m t", m=2)
        ps_tileT = psum[:, 2, :].bitcast(F16).rearrange("p (k t) -> p k t", k=4)
        ps_y = psum[:, 4:8, 0:D].rearrange("p (s c) d -> p s c d", s=2)

        const_in = sem("const_in")
        setup_act = sem("setup_act")
        setup_dve = sem("setup_dve")
        setup_pool = sem("setup_pool")
        x_in = [sem(f"x_in{s}") for s in range(2)]
        w_in = sem("w_in")
        row_out = [sem(f"row_out{s}") for s in range(2)]
        x1_out = [sem(f"x1_out{s}") for s in range(2)]
        zrow_out = sem("zrow_out")
        S = {n: sem(n) for n in (
            "stats1_done", "moments1_done", "ve1_done", "rs1_done", "xn_done", "xT_ps", "xT_done", "xcol_done",
            "res_done", "keys_done", "queries_done", "val_ps", "val_done", "score_ps", "score_done",
            "read_ps", "read_done", "readcol_done", "state_ps", "state_done", "faded_done", "proj_ps",
            "x1_done", "stats2_done", "moments2_done", "ve2_done", "rs2_done", "xm_done", "hi_done", "lo_done",
            "mT_ps", "mT_done", "logit_ps", "logit_done", "top_done", "top_at_done", "shifted_done", "exp_done",
            "pick_done", "mask_done", "esum_done", "rsum_done", "masked_done", "rank_ps", "slots_done",
            "picked_done", "slot_i_done", "base_done", "gates_done", "token_done", "whi_done", "wlo_done")}
        carrier = [sem("carrier_dve"), sem("carrier_pool")]
        table_done = sem("table_done")
        table_step = sem("table_step")
        pad_out = sem("pad_out")
        b2_in = sem("b2_in")
        tile_ld = [sem(f"tile_ld{s}") for s in range(2)]
        S2 = {n: sem(n) for n in ("tileT_ps", "tileT_done", "prep_done", "wcur_done", "h_ps", "act_done",
                                  "hhi_done", "split_done", "l2_done", "ybias_done", "yout_done")}
        added = sem("added")

        block = ctx.enter_context(nc.Block())

        def is_int(n):
            return isinstance(n, int)

        def active(n, lag):
            return not is_int(n) or 0 <= n - lag < NCH

        def reached(eng, name, n):
            if not is_int(n) or n >= 0:
                eng.wait_ge(S[name], n + 1)

        def plainly(eng, *waits):
            for s, v in waits:
                if not is_int(v) or v > 0:
                    eng.wait_ge(s, v)
            if any(not is_int(v) for s, v in waits):
                eng.sem_inc(carrier[eng is nc.gpsimd], 1)

        def loaded(eng, slot_sem, n, par, each=16):
            if not is_int(n) or n >= 0:
                eng.wait_ge(slot_sem, (n - par) * (each // 2) + each)

        def stage_one(eng, step):
            for n in range(PEEL1):
                step(n, n % 2)
            trips = (NCH - 1 - PEEL1) // 2
            with eng.Fori(0, trips) as j:
                step(2 * j + PEEL1, PEEL1 % 2)
                step(2 * j + PEEL1 + 1, (PEEL1 + 1) % 2)
            for n in range(PEEL1 + 2 * trips, NCH + LAG + 1):
                step(n, n % 2)

        def stored(eng):
            for s in range(2):
                eng.wait_ge(x1_out[s], 16 * NCH // 2)
            eng.wait_ge(zrow_out, 16)

        def res_of(n):
            a = (n % 4) * (B * D)
            v = res[:, a:a + B * D] if is_int(a) else res[:, bass.ds(a, B * D)]
            return v.rearrange("p (b d) -> p b d", b=B)

        def both(rows, n):
            v = rows[0:B * T, :].rearrange("(b t) d -> t b d", b=B)
            return v[n * P:(n + 1) * P] if is_int(n) else v[bass.ds(n * P, P)]

        def stage_two(eng, step):
            step(-1, 1)
            step(0, 0)
            step(1, 1)
            trips = (NT - 4) // 2
            with eng.Fori(0, trips) as j:
                step(2 * j + 2, 0)
                step(2 * j + 3, 1)
            for i in range(2 + 2 * trips, NT + 1):
                step(i, i % 2)

        def has(i):
            return not is_int(i) or 0 <= i < NT

        def came(eng, name, i, per=1, k=None):
            if not is_int(i) or i >= 0:
                eng.wait_ge(S2[name], i * per + (per if k is None else k + 1))

        @block.sync
        def _(sp):
            sp.dma_start(consts[:], const).then_inc(const_in, 16)
            sp.dma_start(wwT[:], w_write).then_inc(const_in, 16)
            sp.dma_start(wrT[:], w_read).then_inc(const_in, 16)
            sp.dma_start(gateT[:], gate_w).then_inc(const_in, 16)
            sp.dma_start(b1T[:], b1).then_inc(const_in, 16)
            for src, dst in ((decay, rates), (log_alpha, alphas)):
                heads = src.rearrange("(a h) -> a h", a=1)
                by_side = src.rearrange("(a k s) -> s a k", a=1, s=2)
                sp.dma_start(dst[:, 0:H], heads.to_broadcast([P, H])).then_inc(const_in, 16)
                with nc.allow_non_contiguous_dma(reason="four numbers"):
                    for side in range(2):
                        sp.dma_start(dst[side * HD:(side + 1) * HD, H:H + KD],
                                     by_side[side].to_broadcast([HD, KD])).then_inc(const_in, 16)

            def load_x(n, par):
                reached(sp, "res_done", n - 2)
                reached(sp, "xn_done", n - 2)
                sp.dma_start(xt[:, par], both(x_rows, n)).then_inc(x_in[par], 16)

            load_x(0, 0)

            def step(n, par):
                if active(n + 1, 0):
                    load_x(n + 1, 1 - par)
                if active(n, 0):
                    reached(sp, "whi_done", n - 1)
                    reached(sp, "wlo_done", n - 1)
                    src = experts[2 * n:2 * n + 2] if is_int(n) else experts[bass.ds(2 * n, 2)]
                    sp.dma_start(staged, src.rearrange("a p w -> p a w")).then_inc(w_in, 16)
                if active(n, 3):
                    m = n - 3
                    reached(sp, "x1_done", m)
                    if active(n, 1):
                        reached(sp, "res_done", m + 2)
                    sp.dma_start(both(out, m), res_of(m)).then_inc(x1_out[1 - par], 16)

            stage_one(sp, step)

            sp.wait_ge(setup_pool, 3)
            sp.dma_start(out[TOK:TOK + TILE, :].rearrange("(p c) d -> p (c d)", c=2), zrow).then_inc(zrow_out, 16)
            sp.wait_ge(setup_dve, 12)
            sp.dma_start(sent[E * CAP:E * CAP + TILE, :].rearrange("(p c) w -> p (c w)", c=2),
                         pad[:].rearrange("p c w -> p (c w)")).then_inc(pad_out, 16)
            sp.wait_ge(table_done, 1)
            for s in range(2):
                sp.wait_ge(row_out[s], 64 * NCH // 2)
            reached(sp, "gates_done", NCH - 1)
            stored(sp)
            sp.dma_start(b2_all, b2.rearrange("(a e) d -> a (e d)", a=1).to_broadcast([P, E * D])).then_inc(b2_in, 16)
            for e in range(E):
                r = sp.value_load(pad_row_i[0:1, e:e + 1], min_val=0, max_val=E * CAP - TILE)
                sp.dma_start(sent[bass.ds(r, TILE), :].rearrange("(p c) w -> p (c w)", c=2),
                             pad[:].rearrange("p c w -> p (c w)")).then_inc(pad_out, 16)
            sp.wait_ge(pad_out, 16 * (E + 1))

            def load_tile(i, par):
                came(sp, "tileT_ps", i - 2)
                came(sp, "prep_done", i - 2)
                at_i = tile_row_i[0:1, i:i + 1] if is_int(i) else tile_row_i[0:1, bass.ds(i, 1)]
                r = sp.value_load(at_i, min_val=0, max_val=E * CAP)
                sp.dma_start(tile_in[:, par].rearrange("p c w -> p (c w)"),
                             sent[bass.ds(r, TILE), :].rearrange("(p c) w -> p (c w)", c=2)).then_inc(tile_ld[par], 16)

            def step2(i, par):
                if has(i + 2):
                    load_tile(i + 2, par)

            load_tile(0, 0)
            stage_two(sp, step2)

        @block.gpsimd
        def _(pool):
            pool.memset(minus_half[:], -0.5).then_inc(setup_pool, 1)
            pool.memset(zcol[:], 0.0)
            pool.memset(state[:], 0.0)
            pool.memset(readsT[:, 0, :, :, 0:1], 0.0).then_inc(setup_pool, 1)
            pool.memset(zrow, 0.0).then_inc(setup_pool, 1)
            pool.wait_ge(setup_pool, 1)

            def step(n, par):
                if active(n, 2):
                    m = n - 2
                    reached(pool, "xcol_done", m)
                    reached(pool, "xT_done", m)
                    if is_int(m) and m == 0:
                        pool.wait_ge(setup_act, 8)
                    reached(pool, "read_ps", m - 1)
                    for b in range(B):
                        last = pool.tensor_tensor(queries[:, b], xnT[:, par, b, :, 1:P + 1], decayQ[:], ALU.mult)
                    last.then_inc(S["queries_done"], 1)
                for lag, moments, ve, rs, got, mid, end, used in (
                        (0, moments1, ve1, rs1, "moments1_done", "ve1_done", "rs1_done", "xn_done"),
                        (3, moments2, ve2, rs2, "moments2_done", "ve2_done", "rs2_done", "xm_done")):
                    if active(n, lag):
                        m = n - lag
                        plainly(pool, (S[got], m + 1))
                        pool.tensor_scalar(ve, moments[:, :, 1], EPS, None, ALU.add).then_inc(S[mid], 1)
                        reached(pool, mid, m)
                        reached(pool, used, m - 1)
                        pool.tensor_tensor(rs, ve, minus_half[:].to_broadcast([P, B]), ALU.pow).then_inc(S[end], 1)
                if active(n, 2):
                    m = n - 2
                    reached(pool, "state_done", m - 1)
                    for b in range(B):
                        last = pool.tensor_tensor(faded[:, b], state[:, b],
                                                  decayC[:].unsqueeze(2).to_broadcast([P, KD, P]), ALU.mult)
                    last.then_inc(S["faded_done"], 1)
                if active(n, 0):
                    reached(pool, "xn_done", n)
                    loaded(pool, x_in[par], n, par)
                    loaded(pool, x1_out[par], n - 4, par)
                    pool.tensor_tensor(res_of(n), xt[:, par], xn[:, par], ALU.add).then_inc(S["res_done"], 1)
                if active(n, 1):
                    m = n - 1
                    reached(pool, "xn_done", m)
                    reached(pool, "state_ps", m - 2)
                    for b in range(B):
                        last = pool.tensor_tensor(keys[:, 1 - par, b].rearrange("p (h d) -> p h d", h=H),
                                                  xn[:, 1 - par, b].rearrange("p (h d) -> p h d", h=H),
                                                  decayK[:].unsqueeze(2).to_broadcast([P, H, HD]), ALU.mult)
                    last.then_inc(S["keys_done"], 1)
                if active(n, 4):
                    m = n - 4
                    reached(pool, "hi_done", m)
                    words = row[:, par, :, 0:D].bitcast(F16)
                    pool.tensor_tensor(words[:, :, D:2 * D], xm[:, par], words[:, :, 0:D],
                                       ALU.subtract).then_inc(S["lo_done"], 1)
                if active(n, 5):
                    m, mp = n - 5, 1 - par
                    if is_int(m) and m == 0:
                        pool.wait_ge(setup_dve, 12)
                    src = token_i[:, 2 * m:2 * m + 2] if is_int(m) else token_i[:, bass.ds(2 * m, 2)]
                    pool.tensor_copy(row[:, mp, :, ROW - 1].bitcast(I32), src).then_inc(S["token_done"], 1)
                    plainly(pool, *((S[name], m + 1) for name in
                                    ("token_done", "lo_done", "hi_done", "gates_done", "slot_i_done")))
                    for b in range(B):
                        for k in range(2):
                            at_bk = slot_i[:, 2 * b + k:2 * b + k + 1]
                            pool.indirect_dma_start(
                                out=sent, out_offset=bass.IndirectOffsetOnAxis(ap=at_bk, axis=0),
                                in_=row[:, mp, b, :], in_offset=None).then_inc(row_out[mp], 16)

            stage_one(pool, step)

            stored(pool)

            def step2(i, par):
                if has(i - 1):
                    for c in range(2):
                        plainly(pool, (S2["yout_done"], (i - 1) * 2 + c + 1), (added, (i - 1) * 32 + c * 16))
                        pool.indirect_dma_start(
                            out=out, out_offset=bass.IndirectOffsetOnAxis(ap=tok_cur[:, 1 - par, c:c + 1], axis=0),
                            in_=yout[:, 1 - par, c], in_offset=None, compute_op=ALU.add).then_inc(added, 16)

            stage_two(pool, step2)
            pool.wait_ge(added, 32 * NT)

        @block.scalar
        def _(a):
            a.wait_ge(const_in, 16 * 11)
            a.activation(gam[:], rates[:], ACT.Exp, scale=-1.0).then_inc(setup_act, 1)
            a.wait_ge(setup_dve, 2)
            a.activation(lng[:], gam[:], ACT.Ln).then_inc(setup_act, 1)
            a.wait_ge(setup_act, 2)
            for h in range(H):
                a.activation(decayM[:, h % 2, h // 2, :], const_of("gap"), ACT.Exp, scale=lng[:, h:h + 1],
                             bias=alphas[:, h:h + 1])
            a.activation(decayK[:], lng[:, 0:H], ACT.Exp, scale=const_of("left")).then_inc(setup_act, 1)
            for k in range(KD):
                a.activation(decayQ[:, k, :], const_of("index"), ACT.Exp, scale=lng[:, H + k:H + k + 1],
                             bias=alphas[:, H + k:H + k + 1]).then_inc(setup_act, 1)
            a.activation(decayC[:], lng[:, H:H + KD], ACT.Exp, scale=float(P)).then_inc(setup_act, 1)
            a.activation(ident16[:], ident, ACT.Copy).then_inc(setup_act, 1)
            a.activation(before16[:], before, ACT.Copy).then_inc(setup_act, 1)

            def split_high(n, half):
                if half == 0:
                    a.wait_ge(w_in, 16 * n + 16)
                o = (2 * n + half) * (2 * PIECE)
                dst = weights[:, o:o + PIECE] if is_int(o) else weights[:, bass.ds(o, PIECE)]
                ins = a.activation(dst, staged[:, half], ACT.Copy, scale=WSCALE)
                if half:
                    ins.then_inc(S["whi_done"], 1)

            def step(n, par):
                if active(n, 1):
                    m = n - 1
                    reached(a, "xT_ps", m)
                    reached(a, "score_ps", m - 2)
                    reached(a, "val_ps", m - 2)
                    reached(a, "queries_done", m - 2)
                    a.activation(xnT[:, 1 - par, :, :, 0:P].rearrange("p b k t -> p (b k) t"),
                                 ps_xT.rearrange("p b k t -> p (b k) t"), ACT.Copy).then_inc(S["xT_done"], 1)
                if (active(n, 1) and n - 1 != 0) if is_int(n) else True:
                    a.activation(xnT[:, par, :, :, P:P + 1].rearrange("p b k t -> p (b k) t"),
                                 ps_xT[:, :, :, 0:1].rearrange("p b k t -> p (b k) t"),
                                 ACT.Copy).then_inc(S["xcol_done"], 1)
                if is_int(n) and n - 1 == NCH:
                    a.activation(xnT[:, par, :, :, P:P + 1].rearrange("p b k t -> p (b k) t"),
                                 zcol[:], ACT.Copy).then_inc(S["xcol_done"], 1)
                if active(n, 4):
                    m = n - 4
                    reached(a, "mT_ps", m)
                    reached(a, "logit_ps", m - 1)
                    a.activation(xmT.rearrange("p b k t -> p (b k t)"), ps_mT.rearrange("p b k t -> p (b k t)"),
                                 ACT.Copy).then_inc(S["mT_done"], 1)
                if active(n, 5):
                    m = n - 5
                    reached(a, "shifted_done", m)
                    a.activation(shifted, shifted, ACT.Exp).then_inc(S["exp_done"], 1)
                if active(n, 0):
                    split_high(n, 0)
                if active(n, 2):
                    m = n - 2
                    reached(a, "val_ps", m)
                    reached(a, "state_ps", m - 1)
                    reached(a, "read_ps", m - 1)
                    a.activation(vals, ps_val, ACT.Copy).then_inc(S["val_done"], 1)
                if active(n, 4):
                    m = n - 4
                    reached(a, "xm_done", m)
                    loaded(a, row_out[par], m - 2, par, 64)
                    a.activation(row[:, par, :, 0:D].bitcast(F16)[:, :, 0:D], xm[:, par],
                                 ACT.Copy).then_inc(S["hi_done"], 1)
                if active(n, 0):
                    split_high(n, 1)
                if active(n, 2):
                    m = n - 2
                    reached(a, "read_ps", m)
                    reached(a, "proj_ps", m - 1)
                    a.activation(readsT[:, par, :, :, 1:P + 1].rearrange("p b k t -> p (b k) t"),
                                 ps_read.rearrange("p b k t -> p (b k) t"), ACT.Copy).then_inc(S["read_done"], 1)
                    a.activation(readsT[:, 1 - par, :, :, 0:1].rearrange("p b k t -> p (b k) t"),
                                 ps_read[:, :, :, P - 1:P].rearrange("p b k t -> p (b k) t"),
                                 ACT.Copy).then_inc(S["readcol_done"], 1)

            stage_one(a, step)

            a.wait_ge(table_done, 1)

            def gelu(i, par, pair):
                s = pair % 2
                came(a, "h_ps", i, 4, pair)
                if pair == 0:
                    came(a, "prep_done", i)
                if pair >= 2:
                    came(a, "split_done", i, 4, pair - 2)
                else:
                    came(a, "split_done", i - 1, 4, pair + 2)
                for m in range(2):
                    mm = 2 * pair + m
                    last = a.activation(act[:, s, m * TILE:(m + 1) * TILE], ps_h[:, s, m], ACT.Gelu_apprx_tanh,
                                        scale=1.0 / WSCALE, bias=b1_cur[:, par, mm:mm + 1])
                last.then_inc(S2["act_done"], 1)

            def step2(i, par):
                if has(i):
                    gelu(i, par, 0)
                if has(i - 1):
                    for c in range(2):
                        came(a, "ybias_done", i - 1, 2, c)
                        a.activation(yout[:, 1 - par, c], yout[:, 1 - par, c], ACT.Copy,
                                     scale=gate_cur[:, 1 - par, c:c + 1]).then_inc(S2["yout_done"], 1)
                if has(i):
                    gelu(i, par, 1)
                if has(i + 1):
                    came(a, "tileT_ps", i + 1)
                    came(a, "h_ps", i - 1, 4, 3)
                    a.activation(tileT[:, 1 - par].rearrange("p k t -> p (k t)"),
                                 ps_tileT.rearrange("p k t -> p (k t)"), ACT.Copy).then_inc(S2["tileT_done"], 1)
                if has(i):
                    gelu(i, par, 2)
                    gelu(i, par, 3)

            stage_two(a, step2)

        @block.vector
        def _(v):
            v.wait_ge(setup_act, 1)
            v.tensor_scalar(gam[:], gam[:], 1.0, None, ALU.add).then_inc(setup_dve, 1)
            v.wait_ge(setup_dve, 1)
            v.reciprocal(gam[:], gam[:]).then_inc(setup_dve, 1)
            v.memset(ones16[:], 1.0).then_inc(setup_dve, 1)
            v.tensor_copy(base[:], const_of("region")).then_inc(setup_dve, 1)
            v.tensor_copy(token_i[:], const_of("token")).then_inc(setup_dve, 1)
            v.memset(pad[:], 0.0).then_inc(setup_dve, 1)
            v.wait_ge(setup_dve, 6)
            for c in range(2):
                a0 = CONST["padtoken"][0] + c
                v.tensor_copy(pad[:, c, ROW - 1:ROW].bitcast(I32), consts[:, a0:a0 + 1]).then_inc(setup_dve, 1)
            v.wait_ge(setup_act, 3)
            for side in range(2):
                for k in range(KD):
                    v.tensor_tensor(decayM[:, side, k, :], decayM[:, side, k, :], before, ALU.mult).then_inc(setup_dve, 1)

            v.wait_ge(setup_dve, 12)

            def split_low(n, half):
                if half == 0:
                    reached(v, "whi_done", n)
                    v.wait_ge(w_in, 16 * n + 16)
                o = (2 * n + half) * (2 * PIECE)
                hi = weights[:, o:o + PIECE] if is_int(o) else weights[:, bass.ds(o, PIECE)]
                lo = weights[:, o + PIECE:o + 2 * PIECE] if is_int(o) else weights[:, bass.ds(o + PIECE, PIECE)]
                ins = v.scalar_tensor_tensor(out=lo, in0=staged[:, half], scalar=WSCALE, in1=hi, op0=ALU.mult,
                                             op1=ALU.subtract)
                if half:
                    ins.then_inc(S["wlo_done"], 1)

            def step(n, par):
                if active(n, 5):
                    m = n - 5
                    plainly(v, (S["logit_done"], m + 1))
                    for b in range(B):
                        last = v.max(top[:, b], logit[:, b])
                    last.then_inc(S["top_done"], 1)
                if active(n, 0):
                    plainly(v, (x_in[par], (n - par) * 8 + 16))
                    for b in range(B):
                        last = v.bn_stats(stats1[:, b], xt[:, par, b])
                    last.then_inc(S["stats1_done"], 1)
                if active(n, 5):
                    reached(v, "top_done", m)
                    v.tensor_tensor(shifted, logit, top[:, :, 0:1].to_broadcast([P, B, E]),
                                    ALU.subtract).then_inc(S["shifted_done"], 1)
                    for b in range(B):
                        last = v.max_index(top_at[:, b], top[:, b], logit[:, b])
                    last.then_inc(S["top_at_done"], 1)
                if active(n, 0):
                    plainly(v, (S["stats1_done"], n + 1), (S["ve1_done"], n))
                    for b in range(B):
                        last = v.bn_aggr(moments1[:, b], stats1[:, b])
                    last.then_inc(S["moments1_done"], 1)
                if active(n, 5):
                    reached(v, "top_at_done", m)
                    v.tensor_tensor(pick[:], const_of("experts").unsqueeze(1).unsqueeze(1).to_broadcast([P, B, 2, E]),
                                    top_at[:, :, 0:2].unsqueeze(3).to_broadcast([P, B, 2, E]),
                                    ALU.is_equal).then_inc(S["pick_done"], 1)
                if active(n, 3):
                    m = n - 3
                    reached(v, "proj_ps", m)
                    reached(v, "res_done", m)
                    v.tensor_tensor(res_of(m), ps_proj, res_of(m), ALU.add).then_inc(S["x1_done"], 1)
                if active(n, 5):
                    m = n - 5
                    reached(v, "pick_done", m)
                    reached(v, "rank_ps", m - 1)
                    v.tensor_tensor(mask[:], pick[:, :, 0], pick[:, :, 1], ALU.add).then_inc(S["mask_done"], 1)
                if active(n, 3):
                    m = n - 3
                    plainly(v, (S["x1_done"], m + 1))
                    for b in range(B):
                        last = v.bn_stats(stats2[:, b], res_of(m)[:, b])
                    last.then_inc(S["stats2_done"], 1)
                if active(n, 0):
                    reached(v, "rs1_done", n)
                    reached(v, "xT_ps", n - 2)
                    reached(v, "keys_done", n - 2)
                    reached(v, "res_done", n - 2)
                    for b in range(B):
                        last = v.tensor_scalar(xn[:, par, b], xt[:, par, b], moments1[:, b, 0:1], rs1[:, b:b + 1],
                                               ALU.subtract, ALU.mult)
                    last.then_inc(S["xn_done"], 1)
                if active(n, 3):
                    m = n - 3
                    plainly(v, (S["stats2_done"], m + 1), (S["ve2_done"], m))
                    for b in range(B):
                        last = v.bn_aggr(moments2[:, b], stats2[:, b])
                    last.then_inc(S["moments2_done"], 1)
                if active(n, 2):
                    m = n - 2
                    reached(v, "score_ps", m)
                    reached(v, "read_ps", m - 1)
                    for b in range(B):
                        last = v.tensor_tensor(scores[:, b].rearrange("p s k t -> p s (k t)"), ps_score[:, :, b],
                                               decayM[:].rearrange("p s k t -> p s (k t)"), ALU.mult)
                    last.then_inc(S["score_done"], 1)
                if active(n, 0):
                    split_low(n, 0)
                if active(n, 3):
                    m = n - 3
                    reached(v, "rs2_done", m)
                    reached(v, "mT_ps", m - 2)
                    reached(v, "lo_done", m - 2)
                    for b in range(B):
                        last = v.tensor_scalar(xm[:, 1 - par, b], res_of(m)[:, b], moments2[:, b, 0:1],
                                               rs2[:, b:b + 1], ALU.subtract, ALU.mult)
                    last.then_inc(S["xm_done"], 1)
                if active(n, 5):
                    m, mp = n - 5, 1 - par
                    reached(v, "exp_done", m)
                    v.tensor_reduce(esum, shifted, AX.X, ALU.add).then_inc(S["esum_done"], 1)
                    reached(v, "mask_done", m)
                    v.tensor_tensor(masked, shifted, mask[:], ALU.mult).then_inc(S["masked_done"], 1)
                    reached(v, "rank_ps", m)
                    reached(v, "base_done", m - 1)
                    v.tensor_tensor(slots, ps_rank, base[:].unsqueeze(1).to_broadcast([P, B, E]),
                                    ALU.add).then_inc(S["slots_done"], 1)
                    reached(v, "esum_done", m)
                    v.reciprocal(rsum, esum).then_inc(S["rsum_done"], 1)
                    reached(v, "slots_done", m)
                    v.tensor_tensor(base[:], ps_total, base[:], ALU.add).then_inc(S["base_done"], 1)
                    v.tensor_tensor(picked[:], pick[:], slots.unsqueeze(2).to_broadcast([P, B, 2, E]),
                                    ALU.mult).then_inc(S["picked_done"], 1)
                    reached(v, "rsum_done", m)
                    reached(v, "masked_done", m)
                    reached(v, "lo_done", m)
                    v.tensor_tensor(row[:, mp, :, D:D + E], masked, rsum.unsqueeze(2).to_broadcast([P, B, E]),
                                    ALU.mult).then_inc(S["gates_done"], 1)
                    loaded(v, row_out[par], m - 1, par, 64)
                    reached(v, "picked_done", m)
                    with nc.allow_low_precision(reason="whole numbers below 2**24"):
                        v.tensor_reduce(slot_i, picked[:].rearrange("p b k e -> p (b k) e"), AX.X,
                                        ALU.add).then_inc(S["slot_i_done"], 1)
                if active(n, 2):
                    m = n - 2
                    reached(v, "state_ps", m)
                    reached(v, "faded_done", m)
                    reached(v, "read_ps", m)
                    for side in range(2):
                        d = slice(side * HD, (side + 1) * HD)
                        last = v.tensor_tensor(state[d, :, :, d].rearrange("p b k i -> p (b k) i"),
                                               ps_state[d, :, :, d].rearrange("p b k i -> p (b k) i"),
                                               faded[d, :, :, d].rearrange("p b k i -> p (b k) i"), ALU.add)
                    last.then_inc(S["state_done"], 1)
                if active(n, 4):
                    m = n - 4
                    reached(v, "logit_ps", m)
                    reached(v, "top_at_done", m - 1)
                    v.tensor_copy(logit, ps_logit).then_inc(S["logit_done"], 1)
                if active(n, 0):
                    split_low(n, 1)

            stage_one(v, step)

            count = [0]

            def link(ins):
                count[0] += 1
                ins.then_inc(table_step, 1)
                v.wait_ge(table_step, count[0])

            cnt, tiles, ends = (tab[:, i * E:(i + 1) * E] for i in range(3))
            t_exp, t_end, t_off, t_row, t_cl, t_tmp = (tab[:, 3 * E + i * NT:3 * E + (i + 1) * NT] for i in range(6))
            J = TOK // TILE
            tileno = const_of("tile", 1)
            reached(v, "base_done", NCH - 1)
            v.tensor_copy(pad_row_i, base[0:1, :])
            link(v.tensor_tensor(cnt, base[0:1, :], const_of("region", 1), ALU.subtract))
            c3 = cmp[:, 0:E * J].rearrange("p (e j) -> p e j", e=E)
            link(v.tensor_tensor(c3, cnt.unsqueeze(2).to_broadcast([1, E, J]),
                                 const_of("step", 1).unsqueeze(1).to_broadcast([1, E, J]), ALU.is_gt))
            link(v.tensor_reduce(tiles, c3, AX.X, ALU.add))
            c4 = cmp[:, 0:E * E].rearrange("p (e j) -> p e j", e=E)
            link(v.tensor_tensor(c4, tiles.unsqueeze(1).to_broadcast([1, E, E]),
                                 const_of("upto", 1).rearrange("p (e j) -> p e j", e=E), ALU.mult))
            link(v.tensor_reduce(ends, c4, AX.X, ALU.add))
            c5 = cmp[:, 0:NT * E].rearrange("p (t e) -> p t e", e=E)
            ends_b = ends.unsqueeze(1).to_broadcast([1, NT, E])
            link(v.tensor_tensor(c5, tileno.unsqueeze(2).to_broadcast([1, NT, E]), ends_b, ALU.is_ge))
            link(v.tensor_reduce(t_exp, c5, AX.X, ALU.add))
            link(v.tensor_tensor(c5, c5, ends_b, ALU.mult))
            link(v.tensor_reduce(t_end, c5, AX.X, ALU.max))
            link(v.tensor_tensor(t_off, tileno, t_end, ALU.subtract))
            link(v.tensor_scalar(t_tmp, t_exp, float(CAP), None, ALU.mult))
            link(v.scalar_tensor_tensor(out=t_row, in0=t_off, scalar=float(TILE), in1=t_tmp, op0=ALU.mult, op1=ALU.add))
            link(v.tensor_scalar(t_row, t_row, float(E * CAP), None, ALU.min))
            link(v.tensor_scalar(t_cl, t_exp, float(E - 1), None, ALU.min))
            link(v.tensor_copy(tile_row_i, t_row))
            link(v.tensor_copy(tile_exp_i, t_cl))
            stored(v)
            for s in range(2):
                v.wait_ge(row_out[s], 64 * NCH // 2)
            reached(v, "logit_ps", NCH - 1)
            v.memset(gate_cur[:], 0.0).then_inc(table_done, 1)
            v.wait_ge(table_done, 1)

            def split(i, pair):
                s = pair % 2
                came(v, "act_done", i, 4, pair)
                if pair >= 2:
                    came(v, "l2_done", i, 4, pair - 2)
                else:
                    came(v, "l2_done", i - 1, 4, pair + 2)
                hi = h_hi[:, s].rearrange("p m t -> p (m t)")
                v.tensor_copy(hi, act[:, s]).then_inc(S2["hhi_done"], 1)
                came(v, "hhi_done", i, 4, pair)
                v.tensor_tensor(h_lo[:, s].rearrange("p m t -> p (m t)"), act[:, s], hi,
                                ALU.subtract).then_inc(S2["split_done"], 1)

            def step2(i, par):
                if has(i + 1):
                    at_i = tile_exp_i[0:1, i + 1:i + 2] if is_int(i) else tile_exp_i[0:1, bass.ds(i + 1, 1)]
                    e = v.value_load(at_i, min_val=0, max_val=E - 1)

                def fetch(part):
                    w = 2 * PIECE
                    v.tensor_copy(wcur[:, 1 - par, part * w:(part + 1) * w],
                                  weights[:, bass.ds(e * EW + part * w, w)]).then_inc(S2["wcur_done"], 1)

                if has(i):
                    split(i, 0)
                if has(i - 1):
                    for c in range(2):
                        came(v, "l2_done", i - 1, 4)
                        if is_int(i) and i == 1:
                            v.wait_ge(b2_in, 16)
                        if not is_int(i) or i >= 3:
                            v.wait_ge(added, (i - 2) * 32)
                        v.scalar_tensor_tensor(out=yout[:, 1 - par, c], in0=ps_y[:, 1 - par, c], scalar=1.0 / WSCALE,
                                               in1=b2_cur[:, 1 - par], op0=ALU.mult,
                                               op1=ALU.add).then_inc(S2["ybias_done"], 1)
                for part in range(4):
                    if has(i + 1):
                        if part == 0:
                            came(v, "l2_done", i - 1, 4)
                        fetch(part)
                    if has(i) and part < 3:
                        split(i, part + 1)
                if has(i + 1):
                    v.wait_ge(tile_ld[1 - par], ((i + 1) - (1 - par)) * 8 + 16)
                    if is_int(i) and i == -1:
                        v.wait_ge(b2_in, 16)
                    came(v, "yout_done", i - 1, 2)
                    came(v, "ybias_done", i - 1, 2)
                    if not is_int(i) or i >= 1:
                        v.wait_ge(added, i * 32)
                    v.tensor_copy(b1_cur[:, 1 - par], b1T[:].rearrange("p e m -> p (e m)")[:, bass.ds(e * MF, MF)])
                    v.tensor_copy(b2_cur[:, 1 - par], b2_all[:, bass.ds(e * D, D)])
                    for c in range(2):
                        v.tensor_copy(gate_cur[:, 1 - par, c:c + 1], tile_in[:, 1 - par, c, bass.ds(e + D, 1)])
                    v.tensor_copy(tok_cur[:, 1 - par], tile_in[:, 1 - par, :, ROW - 1].bitcast(I32)).then_inc(
                        S2["prep_done"], 1)

            stage_two(v, step2)

        @block.tensor
        def _(pe):
            pe.wait_ge(const_in, 16 * 11)
            pe.wait_ge(setup_act, 8)
            pe.wait_ge(setup_dve, 12)
            pe.wait_ge(setup_pool, 2)

            def step(n, par):
                if active(n, 1):
                    m = n - 1
                    reached(pe, "xn_done", m)
                    reached(pe, "xT_done", m - 1)
                    reached(pe, "xcol_done", m - 2)
                    if not is_int(n) or n - 6 >= 0:
                        reached(pe, "base_done", n - 6)
                    for b in range(B):
                        for k in range(KD):
                            last = pe.transpose(ps_xT[:, b, k], xn[:, 1 - par, b, k * P:(k + 1) * P], ident)
                    last.then_inc(S["xT_ps"], 1)
                if active(n, 3):
                    m, mp = n - 3, 1 - par
                    reached(pe, "read_done", m)
                    reached(pe, "readcol_done", m - 1)
                    reached(pe, "x1_done", m - 1)
                    for b in range(B):
                        for k in range(KD):
                            last = pe.matmul(ps_proj[:, b], readsT[:, mp, b, k, 0:P], wrT[:, k], start=(k == 0),
                                             stop=(k == KD - 1))
                    last.then_inc(S["proj_ps"], 1)
                if active(n, 4):
                    m = n - 4
                    reached(pe, "xm_done", m)
                    reached(pe, "logit_done", m - 1)
                    for b in range(B):
                        for k in range(KD):
                            last = pe.transpose(ps_mT[:, b, k], xm[:, par, b, k * P:(k + 1) * P], ident)
                    last.then_inc(S["mT_ps"], 1)
                if active(n, 2):
                    m = n - 2
                    reached(pe, "xT_done", m)
                    reached(pe, "xcol_done", m)
                    reached(pe, "score_done", m - 1)
                    for b in range(B):
                        for side in range(2):
                            d = slice(side * HD, (side + 1) * HD)
                            for k in range(KD):
                                last = pe.matmul(ps_score[:, side, b, k * P:(k + 1) * P], xnT[d, par, b, k, 0:P],
                                                 xnT[d, par, b, k, 1:P + 1], start=True, stop=True)
                    last.then_inc(S["score_ps"], 1)
                    reached(pe, "val_done", m - 1)
                    for b in range(B):
                        for k in range(KD):
                            last = pe.matmul(ps_val[:, b], xnT[:, par, b, k, 1:P + 1], wwT[:, k], start=(k == 0),
                                             stop=(k == KD - 1))
                    last.then_inc(S["val_ps"], 1)
                if active(n, 4):
                    m = n - 4
                    reached(pe, "mT_done", m)
                    for b in range(B):
                        for k in range(KD):
                            last = pe.matmul(ps_logit[:, b], xmT[:, b, k], gateT[:, k], start=(k == 0),
                                             stop=(k == KD - 1))
                    last.then_inc(S["logit_ps"], 1)
                if active(n, 5):
                    m = n - 5
                    reached(pe, "mask_done", m)
                    if n - 1 < NCH if is_int(n) else True:
                        reached(pe, "xT_done", n - 1)
                    if (0 < n - 1 < NCH) if is_int(n) else True:
                        reached(pe, "xcol_done", n - 2)
                    pe.matmul(ps_rank, before16[:], mask[:], start=True, stop=True)
                    pe.matmul(ps_rank[:, 1], ones16[:], mask[:, 0], start=False, stop=True, skip_group_check=True)
                    pe.matmul(ps_total, ones16[:], mask[:, 0], start=True, stop=False)
                    pe.matmul(ps_total, ones16[:], mask[:, 1], start=False, stop=True).then_inc(S["rank_ps"], 1)
                if active(n, 2):
                    m = n - 2
                    reached(pe, "keys_done", m)
                    reached(pe, "val_done", m)
                    reached(pe, "state_done", m - 1)
                    for b in range(B):
                        for k in range(KD):
                            last = pe.matmul(ps_state[:, b, k], keys[:, par, b, k * P:(k + 1) * P],
                                             vals[:, b, k * P:(k + 1) * P], start=True, stop=True)
                    last.then_inc(S["state_ps"], 1)
                    reached(pe, "queries_done", m)
                    reached(pe, "score_done", m)
                    reached(pe, "read_done", m - 1)
                    reached(pe, "readcol_done", m - 1)
                    for b in range(B):
                        for k in range(KD):
                            pe.matmul(ps_read[:, b, k], state[:, b, k], queries[:, b, k], start=True, stop=True)
                            for side in range(2):
                                h = 2 * k + side
                                last = pe.matmul(ps_read[side * HD:(side + 1) * HD, b, k],
                                                 vals[:, b, h * HD:(h + 1) * HD], scores[:, b, side, k],
                                                 start=False, stop=True, skip_group_check=True)
                    last.then_inc(S["read_ps"], 1)

            stage_one(pe, step)

            pe.wait_ge(table_done, 1)
            w1_of = lambda par, k, lo, m: wcur[:, par, k * 2 * PIECE + lo * PIECE + m * P:][:, 0:P]
            w2_of = lambda par, m, lo: wcur[:, par, (2 + m // 4) * 2 * PIECE + lo * PIECE + (m % 4) * D:][:, 0:D]

            def first(i, par, pair):
                s = pair % 2
                if pair == 0:
                    came(pe, "wcur_done", i, 4)
                    came(pe, "tileT_done", i)
                if pair >= 2:
                    came(pe, "act_done", i, 4, pair - 2)
                else:
                    came(pe, "act_done", i - 1, 4, pair + 2)
                for mm in range(2):
                    m = 2 * pair + mm
                    n = 0
                    for k in range(KD):
                        for lo, part in ((0, k), (0, KD + k), (1, k)):
                            last = pe.matmul(ps_h[:, s, mm], w1_of(par, k, lo, m), tileT[:, par, part],
                                             start=(n == 0), stop=(n == 3 * KD - 1))
                            n += 1
                last.then_inc(S2["h_ps"], 1)

            def second(i, par, pair):
                s = pair % 2
                came(pe, "split_done", i, 4, pair)
                if pair == 0:
                    came(pe, "ybias_done", i - 2, 2)
                for mm in range(2):
                    m = 2 * pair + mm
                    for c in range(2):
                        hh = h_hi[:, s, mm, c * P:(c + 1) * P]
                        hl = h_lo[:, s, mm, c * P:(c + 1) * P]
                        for n, (lhs, lo) in enumerate(((hh, 0), (hh, 1), (hl, 0))):
                            last = pe.matmul(ps_y[:, par, c], lhs, w2_of(par, m, lo), start=(m == 0 and n == 0),
                                             stop=(m == MF - 1 and n == 2))
                last.then_inc(S2["l2_done"], 1)

            def step2(i, par):
                if has(i):
                    first(i, par, 0)
                if has(i - 1):
                    second(i - 1, 1 - par, 3)
                if has(i):
                    first(i, par, 1)
                if has(i + 1):
                    pe.wait_ge(tile_ld[1 - par], ((i + 1) - (1 - par)) * 8 + 16)
                    came(pe, "tileT_done", i)
                    for part in range(4):
                        for c in range(2):
                            words = tile_in[:, 1 - par, c, 0:D].bitcast(F16)
                            last = pe.transpose(ps_tileT[:, part, c * P:(c + 1) * P],
                                                words[:, part * P:(part + 1) * P], ident16[:])
                    last.then_inc(S2["tileT_ps"], 1)
                if has(i):
                    second(i, par, 0)
                    first(i, par, 2)
                    second(i, par, 1)
                    first(i, par, 3)
                    second(i, par, 2)

            stage_two(pe, step2)


def kernel(L0_attn_out, L0_attn_W_write, L0_attn_W_read, L0_attn_decay, L0_attn_log_alpha,
           L0_ffn_gate_w, L0_ffn_w1, L0_ffn_b1, L0_ffn_w2, L0_ffn_b2):
    import concourse.bacc as bacc
    from concourse.bass_utils import run_bass_kernel_spmd

    blocks = lambda w: np.ascontiguousarray(w.reshape(KD, P, -1).transpose(1, 0, 2))
    w1 = np.asarray(L0_ffn_w1).transpose(1, 2, 0).reshape(E, KD, P, F)
    w2 = np.asarray(L0_ffn_w2).transpose(1, 2, 0).reshape(E, 2, 4, P, D)
    w2 = w2.transpose(0, 1, 3, 2, 4).reshape(E, 2, P, 4 * D)
    arrays = {
        "x": np.ascontiguousarray(L0_attn_out),
        "w_write": blocks(np.asarray(L0_attn_W_write).T),
        "w_read": blocks(np.asarray(L0_attn_W_read).T),
        "decay": np.ascontiguousarray(L0_attn_decay),
        "log_alpha": np.ascontiguousarray(L0_attn_log_alpha),
        "gate_w": blocks(np.asarray(L0_ffn_gate_w).T),
        "experts": np.ascontiguousarray(np.concatenate([w1, w2], axis=1).reshape(NPIECE, P, PIECE)),
        "b1": np.ascontiguousarray(np.asarray(L0_ffn_b1).reshape(E, MF, P).transpose(2, 0, 1)),
        "b2": np.ascontiguousarray(L0_ffn_b2),
        "const": constants(),
    }
    nc = bacc.Bacc("TRN2", target_bir_lowering=False, num_devices=1)
    args = [nc.dram_tensor(f"in_{n}", v.shape, mybir.dt.from_np(v.dtype), kind="ExternalInput").ap()
            for n, v in arrays.items()]
    out = nc.dram_tensor("out", (TOK + TILE, D), F32, kind="ExternalOutput").ap()
    build(nc, *args, out)
    r = run_bass_kernel_spmd(nc, [{f"in_{n}": v for n, v in arrays.items()}], core_ids=[0])
    return np.asarray(r.results[0]["out"])[:TOK].reshape(B, T, D)
```

```python
from contextlib import ExitStack

import numpy as np

import concourse.bass as bass
from concourse import mybir

F32 = mybir.dt.float32
F16 = mybir.dt.float16
BF16 = mybir.dt.bfloat16
I32 = mybir.dt.int32
U32 = mybir.dt.uint32
ALU = mybir.AluOpType
ACT = mybir.ActivationFunctionType
AX = mybir.AxisListType

P = 128
B, T, D = 2, 2048, 256
H, HD = 4, 64
E, F = 8, 1024
KD = D // P
MF = F // P
NCH = T // P
TOK = B * T
EPS = 1e-5
TILE = 256
CAP = TOK + TILE
NT = (2 * TOK + E * (TILE - 1)) // TILE
ROW = D + E + 1
WSCALE = 64.0
PIECE = 1024
NPIECE = E * 4
EW = 4 * PIECE
LAG = 5
PEEL1 = LAG + 2

CONST = {}
_at = 0
for _name, _width in (("ident", P), ("before", P), ("gap", P), ("index", P), ("left", 1), ("experts", E),
                      ("region", E), ("token", 2 * NCH), ("padtoken", 2), ("step", TOK // TILE),
                      ("upto", E * E), ("tile", NT)):
    CONST[_name] = (_at, _width)
    _at += _width
NCONST = _at


def constants():
    c = np.zeros((P, NCONST), np.float32)
    p = np.arange(P)[:, None]
    f = np.arange(P)[None, :]

    def put(name, value):
        a, w = CONST[name]
        c[:, a:a + w] = value

    put("ident", p == f)
    put("before", p < f)
    put("gap", np.maximum(f - 1 - p, 0))
    put("index", f)
    put("left", P - 1 - p)
    put("experts", np.arange(E)[None, :])
    put("region", np.arange(E)[None, :] * CAP)
    q = np.arange(2 * NCH)[None, :]
    put("token", (q % 2) * T + (q // 2) * P + p)
    put("padtoken", TOK + 2 * p + np.arange(2)[None, :])
    put("step", np.arange(TOK // TILE)[None, :] * TILE)
    put("upto", (np.arange(E)[None, :] <= np.arange(E)[:, None]).reshape(1, -1))
    put("tile", np.arange(NT)[None, :])
    return c


def build(nc, x, w_write, w_read, decay, log_alpha, gate_w, experts, b1, b2, const, out):
    with ExitStack() as ctx:
        def sb(name, shape, dt=F32):
            return ctx.enter_context(nc.sbuf_tensor(name, shape, dt))

        def sem(name):
            return ctx.enter_context(nc.semaphore(name))

        sent = nc.dram_tensor("sent_rows", (E * CAP + TILE, ROW), F32, kind="Internal").ap()
        x_rows = x.rearrange("b t d -> (b t) d")

        weights = sb("weights", [P, E * EW])
        consts = sb("consts", [P, NCONST])

        def const_of(name, rows=P):
            a, w = CONST[name]
            return consts[0:rows, a:a + w]

        ident = const_of("ident")
        before = const_of("before")
        ident16 = sb("ident16", [P, P], F16)
        before16 = sb("before16", [P, P], BF16)
        ones16 = sb("ones16", [P, P], BF16)
        wwT = sb("wwT", [P, KD, D])
        wrT = sb("wrT", [P, KD, D])
        gateT = sb("gateT", [P, KD, E])
        gam = sb("gam", [P, H])
        lng = sb("lng", [P, H + KD])
        alphas = sb("alphas", [P, H + KD])
        decayM = sb("decayM", [P, 2, KD, P])
        decayQ = sb("decayQ", [P, KD, P])
        decayK = sb("decayK", [P, H])
        decayC = sb("decayC", [P, KD])
        b1T = sb("b1T", [P, E, MF])
        minus_half = sb("minus_half", [P, 1])
        warm = sb("warm", [P, 1])
        zcol = sb("zcol", [P, B * KD, 1])
        base = sb("base", [P, E])
        token_i = sb("token_i", [P, 2 * NCH], I32)
        pad = sb("pad", [P, 2, ROW])
        tab = sb("tab", [1, 3 * E + 6 * NT])
        cmp = sb("cmp", [1, max(E * TOK // TILE, NT * E)])
        tab_i = sb("tab_i", [1, E + 2 * NT], I32)
        pad_row_i = tab_i[:, 0:E]
        tile_row_i = tab_i[:, E:E + NT]
        tile_exp_i = tab_i[:, E + NT:E + 2 * NT]

        ARENA = 16128
        arena = sb("arena", [P, ARENA])
        at = [0]

        def carve(words):
            a = at[0]
            at[0] += words
            assert at[0] <= ARENA, at[0]
            return arena[:, a:a + words]

        res = carve(4 * 2 * D)
        xt = carve(2 * 2 * D).rearrange("p (s b d) -> p s b d", s=2, b=2)
        xn = carve(2 * 2 * D).rearrange("p (s b d) -> p s b d", s=2, b=2)
        xnT = carve(2 * 2 * KD * (P + 1)).rearrange("p (s b k t) -> p s b k t", s=2, b=2, k=KD)
        keys = carve(2 * 2 * D).rearrange("p (s b d) -> p s b d", s=2, b=2)
        queries = carve(2 * D).rearrange("p (b k t) -> p b k t", b=2, k=KD)
        vals = carve(2 * D).rearrange("p (b d) -> p b d", b=2)
        scores = carve(2 * H * P).rearrange("p (b s k t) -> p b s k t", b=2, s=2, k=KD)
        readsT = carve(2 * 2 * KD * (P + 1)).rearrange("p (s b k t) -> p s b k t", s=2, b=2, k=KD)
        xm = carve(2 * 2 * D).rearrange("p (s b d) -> p s b d", s=2, b=2)
        xmT = carve(2 * D).rearrange("p (b k t) -> p b k t", b=2, k=KD)
        row = carve(2 * 2 * ROW).rearrange("p (s b w) -> p s b w", s=2, b=2)
        state = carve(2 * D).rearrange("p (b k i) -> p b k i", b=2, k=KD)
        end_one = at[0]
        at[0] = 0
        wcur = carve(2 * EW).bitcast(F16).rearrange("p (s w) -> p s w", s=2)
        tile_in = carve(2 * 2 * ROW).rearrange("p (s c w) -> p s c w", s=2, c=2)
        tileT = carve(2 * 4 * TILE // 2).bitcast(F16).rearrange("p (s k t) -> p s k t", s=2, k=4)
        act = carve(2 * 2 * TILE).rearrange("p (s w) -> p s w", s=2)
        h_hi = carve(4 * TILE).bitcast(F16).rearrange("p (s m t) -> p s m t", s=4, m=2)
        h_lo = carve(4 * TILE).bitcast(F16).rearrange("p (s m t) -> p s m t", s=4, m=2)
        yout = carve(2 * 2 * D).rearrange("p (s c d) -> p s c d", s=2, c=2)
        b1_cur = carve(2 * MF).rearrange("p (s m) -> p s m", s=2)
        b2_cur = carve(2 * D).rearrange("p (s d) -> p s d", s=2)
        gate_cur = carve(4).rearrange("p (s c) -> p s c", s=2)
        tok_cur = carve(4).bitcast(I32).rearrange("p (s c) -> p s c", s=2)
        zrow = arena[:, end_one:end_one + 2 * D]
        assert end_one + 2 * D <= ARENA

        small_at = [0]
        tiny = sb("tiny", [P, 176])

        def small(w, dt=F32):
            a = small_at[0]
            small_at[0] += w
            v = tiny[:, a:a + w]
            return v if dt == F32 else v.bitcast(dt)

        by_batch = lambda v: v.rearrange("p (b e) -> p b e", b=B)
        stats1 = by_batch(small(B * 6))
        moments1 = by_batch(small(B * 2))
        ve1, rs1 = small(B), small(B)
        stats2 = by_batch(small(B * 6))
        moments2 = by_batch(small(B * 2))
        ve2, rs2 = small(B), small(B)
        logit = by_batch(small(B * E))
        top = by_batch(small(B * 8))
        top_at = by_batch(small(B * 8, U32))
        shifted = by_batch(small(B * E))
        masked = by_batch(small(B * E))
        esum, rsum = small(B), small(B)
        slot_i = small(2 * B * 2, I32).rearrange("p (s w) -> p s w", s=2)
        slots = by_batch(small(B * E))
        assert small_at[0] <= 176
        pick = sb("pick", [P, B, 2, E])
        picked = sb("picked", [P, B, 2, E])
        mask = sb("mask", [P, B, E], BF16)

        psum = ctx.enter_context(nc.psum_tensor("psum", [P, 8, 512], F32))
        ps_xT = psum[:, 0, :].rearrange("p (b k t) -> p b k t", b=2, k=KD)
        ps_mT = psum[:, 1, :].rearrange("p (b k t) -> p b k t", b=2, k=KD)
        ps_rank = psum[:, 0, 0:B * E].rearrange("p (b e) -> p b e", b=B)
        ps_total = psum[:, 0, B * E:B * E + E]
        ps_logit = psum[:, 1, 0:B * E].rearrange("p (b e) -> p b e", b=B)
        ps_val = psum[:, 2, :].rearrange("p (b d) -> p b d", b=2)
        ps_score = psum[:, 3:5, :].rearrange("p s (b w) -> p s b w", b=2)
        ps_read = psum[:, 5, :].rearrange("p (b k t) -> p b k t", b=2, k=KD)
        ps_state = psum[:, 6, :].rearrange("p (b k i) -> p b k i", b=2, k=KD)
        ps_proj = psum[:, 7, :].rearrange("p (b d) -> p b d", b=2)
        ps_h = psum[:, 0:2, :].rearrange("p s (m t) -> p s m t", m=2)
        ps_tileT = psum[:, 2, :].bitcast(F16).rearrange("p (k t) -> p k t", k=4)
        ps_y = psum[:, 4:8, 0:D].rearrange("p (s c) d -> p s c d", s=2)

        const_in = sem("const_in")
        decay_in = sem("decay_in")
        proj_in = sem("proj_in")
        gate_in = sem("gate_in")
        setup_act = sem("setup_act")
        setup_dve = sem("setup_dve")
        setup_pool = sem("setup_pool")
        x_in = [sem(f"x_in{s}") for s in range(2)]
        w_in = sem("w_in")
        row_out = [sem(f"row_out{s}") for s in range(2)]
        x1_out = [sem(f"x1_out{s}") for s in range(2)]
        zrow_out = sem("zrow_out")
        S = {n: sem(n) for n in (
            "stats1_done", "moments1_done", "ve1_done", "rs1_done", "xn_done", "xT_ps", "xT_done", "xcol_done",
            "res_done", "keys_done", "queries_done", "val_ps", "val_done", "score_ps", "score_done",
            "read_ps", "read_done", "readcol_done", "state_ps", "state_done", "proj_ps",
            "x1_done", "stats2_done", "moments2_done", "ve2_done", "rs2_done", "xm_done", "hi_done", "lo_done",
            "mT_ps", "mT_done", "logit_ps", "logit_done", "top_done", "top_at_done", "shifted_done", "exp_done",
            "pick_done", "mask_done", "esum_done", "rsum_done", "masked_done", "rank_ps", "slots_done",
            "picked_done", "slot_i_done", "base_done", "gates_done", "token_done")}
        carrier = [sem("carrier_dve"), sem("carrier_pool")]
        padrow_done = sem("padrow_done")
        table_done = sem("table_done")
        buffers_free = sem("buffers_free")
        table_step = sem("table_step")
        pad_out = sem("pad_out")
        b2_in = [sem(f"b2_in{s}") for s in range(2)]
        tile_ld = [sem(f"tile_ld{s}") for s in range(2)]
        S2 = {n: sem(n) for n in ("tileT_ps", "tileT_done", "prep_done", "whi_done", "wcur_done", "tok_done", "h_ps", "act_done",
                                  "hhi_done", "split_done", "l2_done", "ybias_done", "yout_done")}
        added = sem("added")

        block = ctx.enter_context(nc.Block())

        def is_int(n):
            return isinstance(n, int)

        def active(n, lag):
            return not is_int(n) or 0 <= n - lag < NCH

        def reached(eng, name, n):
            if not is_int(n) or n >= 0:
                eng.wait_ge(S[name], n + 1)

        def plainly(eng, *waits):
            for s, v in waits:
                if not is_int(v) or v > 0:
                    eng.wait_ge(s, v)
            if any(not is_int(v) for s, v in waits):
                eng.sem_inc(carrier[eng is nc.gpsimd], 1)

        def loaded(eng, slot_sem, n, par, each=16):
            if not is_int(n) or n >= 0:
                eng.wait_ge(slot_sem, (n - par) * (each // 2) + each)

        def stage_one(eng, step):
            for n in range(PEEL1):
                step(n, n % 2)
            trips = (NCH - 1 - PEEL1) // 2
            with eng.Fori(0, trips) as j:
                step(2 * j + PEEL1, PEEL1 % 2)
                step(2 * j + PEEL1 + 1, (PEEL1 + 1) % 2)
            for n in range(PEEL1 + 2 * trips, NCH + LAG + 1):
                step(n, n % 2)

        def stored(eng):
            for s in range(2):
                eng.wait_ge(x1_out[s], 16 * NCH // 2)
            eng.wait_ge(zrow_out, 16)

        def res_of(n):
            a = (n % 4) * (B * D)
            v = res[:, a:a + B * D] if is_int(a) else res[:, bass.ds(a, B * D)]
            return v.rearrange("p (b d) -> p b d", b=B)

        def both(rows, n):
            v = rows[0:B * T, :].rearrange("(b t) d -> t b d", b=B)
            return v[n * P:(n + 1) * P] if is_int(n) else v[bass.ds(n * P, P)]

        def stage_two(eng, step):
            step(-1, 1)
            step(0, 0)
            step(1, 1)
            trips = (NT - 4) // 2
            with eng.Fori(0, trips) as j:
                step(2 * j + 2, 0)
                step(2 * j + 3, 1)
            for i in range(2 + 2 * trips, NT + 1):
                step(i, i % 2)

        def has(i):
            return not is_int(i) or 0 <= i < NT

        def came(eng, name, i, per=1, k=None):
            if not is_int(i) or i >= 0:
                eng.wait_ge(S2[name], i * per + (per if k is None else k + 1))

        @block.sync
        def _(sp):
            def load_x(n, par):
                reached(sp, "res_done", n - 2)
                reached(sp, "xn_done", n - 2)
                sp.dma_start(xt[:, par], both(x_rows, n)).then_inc(x_in[par], 16)

            for src, dst in ((decay, gam), (log_alpha, alphas)):
                sp.dma_start(dst[:, 0:H], src.rearrange("(a h) -> a h", a=1).to_broadcast([P, H])).then_inc(decay_in, 16)
            load_x(0, 0)
            sp.dma_start(consts[:], const).then_inc(const_in, 16)
            load_x(1, 1)
            sp.dma_start(wwT[:], w_write).then_inc(proj_in, 16)
            sp.dma_start(wrT[:], w_read).then_inc(proj_in, 16)
            sp.dma_start(gateT[:], gate_w).then_inc(gate_in, 16)
            sp.dma_start(b1T[:], b1).then_inc(gate_in, 16)

            def step(n, par):
                if (active(n + 1, 0) and n > 0) if is_int(n) else True:
                    load_x(n + 1, 1 - par)
                if active(n, 0):
                    src = experts[2 * n:2 * n + 2] if is_int(n) else experts[bass.ds(2 * n, 2)]
                    o = 2 * n * PIECE
                    dst = weights[:, o:o + 2 * PIECE] if is_int(n) else weights[:, bass.ds(o, 2 * PIECE)]
                    sp.dma_start(dst.rearrange("p (a w) -> p a w", a=2),
                                 src.rearrange("a p w -> p a w")).then_inc(w_in, 16)
                if active(n, 3):
                    m = n - 3
                    reached(sp, "x1_done", m)
                    if active(n, 1):
                        reached(sp, "res_done", m + 2)
                    sp.dma_start(both(out, m), res_of(m)).then_inc(x1_out[1 - par], 16)

            stage_one(sp, step)

            sp.wait_ge(setup_pool, 3)
            sp.dma_start(out[TOK:TOK + TILE, :].rearrange("(p c) d -> p (c d)", c=2), zrow).then_inc(zrow_out, 16)
            sp.wait_ge(setup_dve, 17)
            sp.dma_start(sent[E * CAP:E * CAP + TILE, :].rearrange("(p c) w -> p (c w)", c=2),
                         pad[:].rearrange("p c w -> p (c w)")).then_inc(pad_out, 16)
            sp.wait_ge(padrow_done, 1)
            for e in range(E):
                r = sp.value_load(pad_row_i[0:1, e:e + 1], min_val=0, max_val=E * CAP - TILE)
                sp.dma_start(sent[bass.ds(r, TILE), :].rearrange("(p c) w -> p (c w)", c=2),
                             pad[:].rearrange("p c w -> p (c w)")).then_inc(pad_out, 16)
            sp.wait_ge(table_done, 1)
            r0 = sp.value_load(tile_row_i[0:1, 0:1], min_val=0, max_val=E * CAP)
            for s in range(2):
                sp.wait_ge(row_out[s], 64 * NCH // 2)
            reached(sp, "gates_done", NCH - 1)
            stored(sp)
            sp.wait_ge(pad_out, 16 * (E + 1))

            def load_tile(i, par):
                came(sp, "tileT_ps", i - 2)
                came(sp, "prep_done", i - 2)
                came(sp, "tok_done", i - 2)
                at_i = tile_row_i[0:1, i:i + 1] if is_int(i) else tile_row_i[0:1, bass.ds(i, 1)]
                r = r0 if is_int(i) and i == 0 else sp.value_load(at_i, min_val=0, max_val=E * CAP)
                sp.dma_start(tile_in[:, par].rearrange("p c w -> p (c w)"),
                             sent[bass.ds(r, TILE), :].rearrange("(p c) w -> p (c w)", c=2)).then_inc(tile_ld[par], 16)
                came(sp, "ybias_done", i - 2, 2)
                at_i = tile_exp_i[0:1, i:i + 1] if is_int(i) else tile_exp_i[0:1, bass.ds(i, 1)]
                e = sp.value_load(at_i, min_val=0, max_val=E - 1)
                sp.dma_start(b2_cur[:, par], b2[bass.ds(e, 1), :].to_broadcast([P, D])).then_inc(b2_in[par], 16)

            def step2(i, par):
                if has(i + 1):
                    load_tile(i + 1, 1 - par)

            stage_two(sp, step2)

        @block.gpsimd
        def _(pool):
            pool.memset(minus_half[:], -0.5).then_inc(setup_pool, 1)
            pool.memset(zcol[:], 0.0)
            pool.memset(state[:], 0.0)
            pool.memset(readsT[:, 0, :, :, 0:1], 0.0).then_inc(setup_pool, 1)
            pool.memset(zrow, 0.0).then_inc(setup_pool, 1)
            pool.memset(pad[:], 0.0).then_inc(setup_pool, 1)
            pool.wait_ge(setup_pool, 1)

            def step(n, par):
                for lag, moments, ve, rs, got, mid, end, used in (
                        (0, moments1, ve1, rs1, "moments1_done", "ve1_done", "rs1_done", "xn_done"),
                        (3, moments2, ve2, rs2, "moments2_done", "ve2_done", "rs2_done", "xm_done")):
                    if active(n, lag):
                        m = n - lag
                        plainly(pool, (S[got], m + 1))
                        pool.tensor_scalar(ve, moments[:, :, 1], EPS, None, ALU.add).then_inc(S[mid], 1)
                        reached(pool, mid, m)
                        reached(pool, used, m - 1)
                        pool.tensor_tensor(rs, ve, minus_half[:].to_broadcast([P, B]), ALU.pow).then_inc(S[end], 1)
                if active(n, 0):
                    reached(pool, "xn_done", n)
                    loaded(pool, x_in[par], n, par)
                    loaded(pool, x1_out[par], n - 4, par)
                    pool.tensor_tensor(res_of(n), xt[:, par], xn[:, par], ALU.add).then_inc(S["res_done"], 1)
                if active(n, 5):
                    m, mp = n - 5, 1 - par
                    if is_int(m) and m == 0:
                        pool.wait_ge(setup_dve, 17)
                    src = token_i[:, 2 * m:2 * m + 2] if is_int(m) else token_i[:, bass.ds(2 * m, 2)]
                    pool.tensor_copy(row[:, mp, :, ROW - 1].bitcast(I32), src).then_inc(S["token_done"], 1)
                    plainly(pool, *((S[name], m + 1) for name in
                                    ("token_done", "lo_done", "hi_done", "gates_done", "slot_i_done")))
                    for b in range(B):
                        for k in range(2):
                            at_bk = slot_i[:, mp, 2 * b + k:2 * b + k + 1]
                            pool.indirect_dma_start(
                                out=sent, out_offset=bass.IndirectOffsetOnAxis(ap=at_bk, axis=0),
                                in_=row[:, mp, b, :], in_offset=None).then_inc(row_out[mp], 16)
                if active(n, 4):
                    m = n - 4
                    reached(pool, "hi_done", m)
                    words = row[:, par, :, 0:D].bitcast(F16)
                    pool.tensor_tensor(words[:, :, D:2 * D], xm[:, par], words[:, :, 0:D],
                                       ALU.subtract).then_inc(S["lo_done"], 1)

            stage_one(pool, step)

            stored(pool)

            def step2(i, par):
                if is_int(i) and i == -1:
                    copy_tokens(0, 0)
                if has(i - 1):
                    for c in range(2):
                        plainly(pool, (S2["yout_done"], (i - 1) * 2 + c + 1), (S2["tok_done"], i),
                                (added, (i - 1) * 32))
                        pool.indirect_dma_start(
                            out=out, out_offset=bass.IndirectOffsetOnAxis(ap=tok_cur[:, 1 - par, c:c + 1], axis=0),
                            in_=yout[:, 1 - par, c], in_offset=None, compute_op=ALU.add).then_inc(added, 16)
                if has(i) and has(i + 1):
                    copy_tokens(i + 1, 1 - par)

            def copy_tokens(i, par):
                plainly(pool, (tile_ld[par], (i - par) * 8 + 16), (added, (i - 1) * 32))
                pool.tensor_copy(tok_cur[:, par], tile_in[:, par, :, ROW - 1].bitcast(I32)).then_inc(S2["tok_done"], 1)

            stage_two(pool, step2)
            pool.wait_ge(added, 32 * NT)

        @block.scalar
        def _(a):
            a.wait_ge(decay_in, 32)
            a.activation(gam[:], gam[:], ACT.Exp, scale=-1.0).then_inc(setup_act, 1)
            a.wait_ge(setup_dve, 2)
            a.activation(lng[:, 0:H], gam[:], ACT.Ln).then_inc(setup_act, 1)
            a.wait_ge(setup_act, 2)
            a.wait_ge(const_in, 16)
            for h in range(H):
                a.activation(decayM[:, h % 2, h // 2, :], const_of("gap"), ACT.Exp, scale=lng[:, h:h + 1],
                             bias=alphas[:, h:h + 1])
            a.activation(decayK[:], lng[:, 0:H], ACT.Exp, scale=const_of("left")).then_inc(setup_act, 1)
            a.wait_ge(setup_dve, 6)
            for k in range(KD):
                a.activation(decayQ[:, k, :], const_of("index"), ACT.Exp, scale=lng[:, H + k:H + k + 1],
                             bias=alphas[:, H + k:H + k + 1]).then_inc(setup_act, 1)
            a.activation(decayC[:], lng[:, H:H + KD], ACT.Exp, scale=float(P)).then_inc(setup_act, 1)
            a.wait_ge(setup_act, 6)

            def step(n, par):
                if active(n, 1):
                    m = n - 1
                    reached(a, "xn_done", m)
                    reached(a, "state_ps", m - 2)
                    for h in range(H):
                        d = slice(h * HD, (h + 1) * HD)
                        last = a.activation(keys[:, 1 - par, :, d], xn[:, 1 - par, :, d], ACT.Copy,
                                            scale=decayK[:, h:h + 1])
                    last.then_inc(S["keys_done"], 1)
                if active(n, 1):
                    m = n - 1
                    reached(a, "xT_ps", m)
                    reached(a, "score_ps", m - 2)
                    reached(a, "val_ps", m - 2)
                    reached(a, "queries_done", m - 2)
                    a.activation(xnT[:, 1 - par, :, :, 0:P].rearrange("p b k t -> p (b k) t"),
                                 ps_xT.rearrange("p b k t -> p (b k) t"), ACT.Copy).then_inc(S["xT_done"], 1)
                if (active(n, 1) and n - 1 != 0) if is_int(n) else True:
                    a.activation(xnT[:, par, :, :, P:P + 1].rearrange("p b k t -> p (b k) t"),
                                 ps_xT[:, :, :, 0:1].rearrange("p b k t -> p (b k) t"),
                                 ACT.Copy).then_inc(S["xcol_done"], 1)
                if is_int(n) and n - 1 == NCH:
                    a.activation(xnT[:, par, :, :, P:P + 1].rearrange("p b k t -> p (b k) t"),
                                 zcol[:], ACT.Copy).then_inc(S["xcol_done"], 1)
                if active(n, 4):
                    m = n - 4
                    reached(a, "mT_ps", m)
                    reached(a, "logit_ps", m - 1)
                    a.activation(xmT.rearrange("p b k t -> p (b k t)"), ps_mT.rearrange("p b k t -> p (b k t)"),
                                 ACT.Copy).then_inc(S["mT_done"], 1)
                if active(n, 5):
                    m = n - 5
                    reached(a, "shifted_done", m)
                    a.activation(shifted, shifted, ACT.Exp).then_inc(S["exp_done"], 1)
                if active(n, 2):
                    m = n - 2
                    reached(a, "val_ps", m)
                    reached(a, "state_ps", m - 1)
                    reached(a, "read_ps", m - 1)
                    a.activation(vals, ps_val, ACT.Copy).then_inc(S["val_done"], 1)
                if active(n, 4):
                    m = n - 4
                    reached(a, "xm_done", m)
                    loaded(a, row_out[par], m - 2, par, 64)
                    a.activation(row[:, par, :, 0:D].bitcast(F16)[:, :, 0:D], xm[:, par],
                                 ACT.Copy).then_inc(S["hi_done"], 1)
                if active(n, 2):
                    m = n - 2
                    reached(a, "read_ps", m)
                    reached(a, "proj_ps", m - 1)
                    a.activation(readsT[:, par, :, :, 1:P + 1].rearrange("p b k t -> p (b k) t"),
                                 ps_read.rearrange("p b k t -> p (b k) t"), ACT.Copy).then_inc(S["read_done"], 1)
                    a.activation(readsT[:, 1 - par, :, :, 0:1].rearrange("p b k t -> p (b k) t"),
                                 ps_read[:, :, :, P - 1:P].rearrange("p b k t -> p (b k) t"),
                                 ACT.Copy).then_inc(S["readcol_done"], 1)

            stage_one(a, step)

            a.wait_ge(table_done, 1)

            def gelu(i, par, pair):
                s = pair % 2
                came(a, "h_ps", i, 4, pair)
                if pair == 0:
                    came(a, "prep_done", i)
                if pair >= 2:
                    came(a, "split_done", i, 4, pair - 2)
                else:
                    came(a, "split_done", i - 1, 4, pair + 2)
                for m in range(2):
                    mm = 2 * pair + m
                    last = a.activation(act[:, s, m * TILE:(m + 1) * TILE], ps_h[:, s, m], ACT.Gelu_apprx_tanh,
                                        scale=1.0 / WSCALE, bias=b1_cur[:, par, mm:mm + 1])
                last.then_inc(S2["act_done"], 1)

            def step2(i, par):
                if has(i + 1):
                    at_i = tile_exp_i[0:1, i + 1:i + 2] if is_int(i) else tile_exp_i[0:1, bass.ds(i + 1, 1)]
                    e = a.value_load(at_i, min_val=0, max_val=E - 1)
                    if is_int(i) and i == -1:
                        a.wait_ge(buffers_free, 1)

                def split_high(part):
                    if part == 0:
                        came(a, "h_ps", i - 1, 4)
                        if is_int(i) and i == -1:
                            a.wait_ge(w_in, 16 * NCH)
                    if part == 2:
                        came(a, "l2_done", i - 1, 4)
                    w = 2 * part * PIECE
                    a.activation(wcur[:, 1 - par, w:w + PIECE], weights[:, bass.ds(e * EW + part * PIECE, PIECE)],
                                 ACT.Copy, scale=WSCALE).then_inc(S2["whi_done"], 1)

                if has(i + 1):
                    split_high(0)
                if has(i):
                    gelu(i, par, 0)
                if has(i + 1):
                    split_high(1)
                if has(i):
                    gelu(i, par, 1)
                if has(i + 1):
                    split_high(2)
                if has(i):
                    gelu(i, par, 2)
                if has(i - 1):
                    for c in range(2):
                        came(a, "ybias_done", i - 1, 2, c)
                        a.activation(yout[:, 1 - par, c], yout[:, 1 - par, c], ACT.Copy,
                                     scale=gate_cur[:, 1 - par, c:c + 1]).then_inc(S2["yout_done"], 1)
                if has(i + 1):
                    if is_int(i) and i == -1:
                        a.activation(warm[:], minus_half[:], ACT.Gelu_apprx_tanh)
                    came(a, "tileT_ps", i + 1)
                    a.activation(tileT[:, 1 - par].rearrange("p k t -> p (k t)"),
                                 ps_tileT.rearrange("p k t -> p (k t)"), ACT.Copy).then_inc(S2["tileT_done"], 1)
                    split_high(3)
                if has(i):
                    gelu(i, par, 3)

            stage_two(a, step2)

        @block.vector
        def _(v):
            v.wait_ge(setup_act, 1)
            v.tensor_scalar(gam[:], gam[:], 1.0, None, ALU.add).then_inc(setup_dve, 1)
            v.wait_ge(setup_dve, 1)
            v.reciprocal(gam[:], gam[:]).then_inc(setup_dve, 1)
            for got, table in ((1, alphas), (2, lng)):
                v.wait_ge(setup_act, got)
                for side in range(2):
                    rows = slice(side * HD, (side + 1) * HD)
                    v.tensor_copy(table[rows, H:H + KD],
                                  table[rows, 0:H].rearrange("p (k s) -> p k s", s=2)[:, :, side]).then_inc(setup_dve, 1)
            v.memset(ones16[:], 1.0).then_inc(setup_dve, 1)
            v.wait_ge(const_in, 16)
            v.tensor_copy(base[:], const_of("region")).then_inc(setup_dve, 1)
            v.tensor_copy(token_i[:], const_of("token")).then_inc(setup_dve, 1)
            v.tensor_copy(ident16[:], ident).then_inc(setup_dve, 1)
            v.tensor_copy(before16[:], before).then_inc(setup_dve, 1)
            v.wait_ge(setup_pool, 4)
            for c in range(2):
                a0 = CONST["padtoken"][0] + c
                v.tensor_copy(pad[:, c, ROW - 1:ROW].bitcast(I32), consts[:, a0:a0 + 1]).then_inc(setup_dve, 1)

            v.wait_ge(setup_dve, 13)

            def step(n, par):
                if active(n, 5):
                    m = n - 5
                    plainly(v, (S["logit_done"], m + 1))
                    for b in range(B):
                        last = v.max(top[:, b], logit[:, b])
                    last.then_inc(S["top_done"], 1)
                if active(n, 0):
                    plainly(v, (x_in[par], (n - par) * 8 + 16))
                    for b in range(B):
                        last = v.bn_stats(stats1[:, b], xt[:, par, b])
                    last.then_inc(S["stats1_done"], 1)
                if active(n, 5):
                    reached(v, "top_done", m)
                    v.tensor_tensor(shifted, logit, top[:, :, 0:1].to_broadcast([P, B, E]),
                                    ALU.subtract).then_inc(S["shifted_done"], 1)
                    for b in range(B):
                        last = v.max_index(top_at[:, b], top[:, b], logit[:, b])
                    last.then_inc(S["top_at_done"], 1)
                if active(n, 0):
                    plainly(v, (S["stats1_done"], n + 1), (S["ve1_done"], n))
                    for b in range(B):
                        last = v.bn_aggr(moments1[:, b], stats1[:, b])
                    last.then_inc(S["moments1_done"], 1)
                if active(n, 5):
                    reached(v, "top_at_done", m)
                    v.tensor_tensor(pick[:], const_of("experts").unsqueeze(1).unsqueeze(1).to_broadcast([P, B, 2, E]),
                                    top_at[:, :, 0:2].unsqueeze(3).to_broadcast([P, B, 2, E]),
                                    ALU.is_equal).then_inc(S["pick_done"], 1)
                if active(n, 3):
                    m = n - 3
                    reached(v, "proj_ps", m)
                    reached(v, "res_done", m)
                    v.tensor_tensor(res_of(m), ps_proj, res_of(m), ALU.add).then_inc(S["x1_done"], 1)
                if active(n, 5):
                    m = n - 5
                    reached(v, "pick_done", m)
                    reached(v, "rank_ps", m - 1)
                    v.tensor_tensor(mask[:], pick[:, :, 0], pick[:, :, 1], ALU.add).then_inc(S["mask_done"], 1)
                if active(n, 3):
                    m = n - 3
                    plainly(v, (S["x1_done"], m + 1))
                    for b in range(B):
                        last = v.bn_stats(stats2[:, b], res_of(m)[:, b])
                    last.then_inc(S["stats2_done"], 1)
                if active(n, 2):
                    m = n - 2
                    reached(v, "xcol_done", m)
                    reached(v, "xT_done", m)
                    if is_int(m) and m == 0:
                        v.wait_ge(setup_act, 6)
                    reached(v, "read_ps", m - 1)
                    for b in range(B):
                        last = v.tensor_tensor(queries[:, b], xnT[:, par, b, :, 1:P + 1], decayQ[:], ALU.mult)
                    last.then_inc(S["queries_done"], 1)
                if active(n, 0):
                    reached(v, "rs1_done", n)
                    reached(v, "xT_ps", n - 2)
                    reached(v, "keys_done", n - 2)
                    reached(v, "res_done", n - 2)
                    for b in range(B):
                        last = v.tensor_scalar(xn[:, par, b], xt[:, par, b], moments1[:, b, 0:1], rs1[:, b:b + 1],
                                               ALU.subtract, ALU.mult)
                    last.then_inc(S["xn_done"], 1)
                if active(n, 3):
                    m = n - 3
                    plainly(v, (S["stats2_done"], m + 1), (S["ve2_done"], m))
                    for b in range(B):
                        last = v.bn_aggr(moments2[:, b], stats2[:, b])
                    last.then_inc(S["moments2_done"], 1)
                if active(n, 2):
                    m = n - 2
                    if is_int(m) and m == 0:
                        v.wait_ge(setup_act, 3)
                        for side in range(2):
                            for k in range(KD):
                                v.tensor_tensor(decayM[:, side, k, :], decayM[:, side, k, :], before,
                                                ALU.mult).then_inc(setup_dve, 1)
                        v.wait_ge(setup_dve, 17)
                    reached(v, "score_ps", m)
                    reached(v, "read_ps", m - 1)
                    for b in range(B):
                        last = v.tensor_tensor(scores[:, b].rearrange("p s k t -> p s (k t)"), ps_score[:, :, b],
                                               decayM[:].rearrange("p s k t -> p s (k t)"), ALU.mult)
                    last.then_inc(S["score_done"], 1)
                if active(n, 4):
                    m = n - 4
                    reached(v, "logit_ps", m)
                    reached(v, "top_at_done", m - 1)
                    v.tensor_copy(logit, ps_logit).then_inc(S["logit_done"], 1)
                if active(n, 3):
                    m = n - 3
                    reached(v, "rs2_done", m)
                    reached(v, "mT_ps", m - 2)
                    reached(v, "lo_done", m - 2)
                    for b in range(B):
                        last = v.tensor_scalar(xm[:, 1 - par, b], res_of(m)[:, b], moments2[:, b, 0:1],
                                               rs2[:, b:b + 1], ALU.subtract, ALU.mult)
                    last.then_inc(S["xm_done"], 1)
                if active(n, 5):
                    m, mp = n - 5, 1 - par
                    reached(v, "exp_done", m)
                    v.tensor_reduce(esum, shifted, AX.X, ALU.add).then_inc(S["esum_done"], 1)
                    reached(v, "mask_done", m)
                    v.tensor_tensor(masked, shifted, mask[:], ALU.mult).then_inc(S["masked_done"], 1)
                    reached(v, "rank_ps", m)
                    reached(v, "base_done", m - 1)
                    v.tensor_tensor(slots, ps_rank, base[:].unsqueeze(1).to_broadcast([P, B, E]),
                                    ALU.add).then_inc(S["slots_done"], 1)
                    reached(v, "esum_done", m)
                    v.reciprocal(rsum, esum).then_inc(S["rsum_done"], 1)
                    reached(v, "slots_done", m)
                    v.tensor_tensor(base[:], ps_total, base[:], ALU.add).then_inc(S["base_done"], 1)
                    v.tensor_tensor(picked[:], pick[:], slots.unsqueeze(2).to_broadcast([P, B, 2, E]),
                                    ALU.mult).then_inc(S["picked_done"], 1)
                    reached(v, "rsum_done", m)
                    reached(v, "masked_done", m)
                    loaded(v, row_out[mp], m - 2, mp, 64)
                    v.tensor_tensor(row[:, mp, :, D:D + E], masked, rsum.unsqueeze(2).to_broadcast([P, B, E]),
                                    ALU.mult).then_inc(S["gates_done"], 1)
                    reached(v, "picked_done", m)
                    with nc.allow_low_precision(reason="whole numbers below 2**24"):
                        v.tensor_reduce(slot_i[:, mp], picked[:].rearrange("p b k e -> p (b k) e"), AX.X,
                                        ALU.add).then_inc(S["slot_i_done"], 1)
                if active(n, 2):
                    m = n - 2
                    reached(v, "state_ps", m)
                    reached(v, "read_ps", m)
                    for side in range(2):
                        d = slice(side * HD, (side + 1) * HD)
                        for k in range(KD):
                            last = v.scalar_tensor_tensor(out=state[d, :, k, d], in0=state[d, :, k, d],
                                                          scalar=decayC[d, k:k + 1], in1=ps_state[d, :, k, d],
                                                          op0=ALU.mult, op1=ALU.add)
                    last.then_inc(S["state_done"], 1)

            stage_one(v, step)

            count = [0]

            def link(ins):
                count[0] += 1
                ins.then_inc(table_step, 1)
                v.wait_ge(table_step, count[0])

            cnt, tiles, ends = (tab[:, i * E:(i + 1) * E] for i in range(3))
            t_exp, t_end, t_off, t_row, t_cl, t_tmp = (tab[:, 3 * E + i * NT:3 * E + (i + 1) * NT] for i in range(6))
            J = TOK // TILE
            tileno = const_of("tile", 1)
            reached(v, "base_done", NCH - 1)
            v.tensor_copy(pad_row_i, base[0:1, :]).then_inc(padrow_done, 1)
            link(v.tensor_tensor(cnt, base[0:1, :], const_of("region", 1), ALU.subtract))
            c3 = cmp[:, 0:E * J].rearrange("p (e j) -> p e j", e=E)
            link(v.tensor_tensor(c3, cnt.unsqueeze(2).to_broadcast([1, E, J]),
                                 const_of("step", 1).unsqueeze(1).to_broadcast([1, E, J]), ALU.is_gt))
            link(v.tensor_reduce(tiles, c3, AX.X, ALU.add))
            c4 = cmp[:, 0:E * E].rearrange("p (e j) -> p e j", e=E)
            link(v.tensor_tensor(c4, tiles.unsqueeze(1).to_broadcast([1, E, E]),
                                 const_of("upto", 1).rearrange("p (e j) -> p e j", e=E), ALU.mult))
            link(v.tensor_reduce(ends, c4, AX.X, ALU.add))
            c5 = cmp[:, 0:NT * E].rearrange("p (t e) -> p t e", e=E)
            ends_b = ends.unsqueeze(1).to_broadcast([1, NT, E])
            link(v.tensor_tensor(c5, tileno.unsqueeze(2).to_broadcast([1, NT, E]), ends_b, ALU.is_ge))
            link(v.tensor_reduce(t_exp, c5, AX.X, ALU.add))
            link(v.tensor_tensor(c5, c5, ends_b, ALU.mult))
            link(v.tensor_reduce(t_end, c5, AX.X, ALU.max))
            link(v.tensor_tensor(t_off, tileno, t_end, ALU.subtract))
            link(v.tensor_scalar(t_tmp, t_exp, float(CAP), None, ALU.mult))
            link(v.scalar_tensor_tensor(out=t_row, in0=t_off, scalar=float(TILE), in1=t_tmp, op0=ALU.mult, op1=ALU.add))
            link(v.tensor_scalar(t_row, t_row, float(E * CAP), None, ALU.min))
            link(v.tensor_scalar(t_cl, t_exp, float(E - 1), None, ALU.min))
            link(v.tensor_copy(tile_row_i, t_row))
            link(v.tensor_copy(tile_exp_i, t_cl))
            v.sem_inc(table_done, 1)
            stored(v)
            for s in range(2):
                v.wait_ge(row_out[s], 64 * NCH // 2)
            reached(v, "logit_ps", NCH - 1)
            v.sem_inc(buffers_free, 1)

            def split(i, pair):
                came(v, "act_done", i, 4, pair)
                came(v, "l2_done", i - 1, 4, pair)
                hi = h_hi[:, pair].rearrange("p m t -> p (m t)")
                v.tensor_copy(hi, act[:, pair % 2]).then_inc(S2["hhi_done"], 1)
                came(v, "hhi_done", i, 4, pair)
                v.tensor_tensor(h_lo[:, pair].rearrange("p m t -> p (m t)"), act[:, pair % 2], hi,
                                ALU.subtract).then_inc(S2["split_done"], 1)

            def step2(i, par):
                if has(i + 1):
                    at_i = tile_exp_i[0:1, i + 1:i + 2] if is_int(i) else tile_exp_i[0:1, bass.ds(i + 1, 1)]
                    e = v.value_load(at_i, min_val=0, max_val=E - 1)

                def split_low(part):
                    came(v, "whi_done", i + 1, 4, part)
                    w = 2 * part * PIECE
                    v.scalar_tensor_tensor(out=wcur[:, 1 - par, w + PIECE:w + 2 * PIECE],
                                           in0=weights[:, bass.ds(e * EW + part * PIECE, PIECE)], scalar=WSCALE,
                                           in1=wcur[:, 1 - par, w:w + PIECE], op0=ALU.mult,
                                           op1=ALU.subtract).then_inc(S2["wcur_done"], 1)

                if has(i + 1):
                    split_low(0)
                if has(i):
                    split(i, 0)
                if has(i + 1):
                    split_low(1)
                if has(i):
                    split(i, 1)
                if has(i - 1):
                    for c in range(2):
                        came(v, "l2_done", i - 1, 4)
                        v.wait_ge(b2_in[1 - par], (i - 1 - (1 - par)) * 8 + 16)
                        if not is_int(i) or i >= 3:
                            v.wait_ge(added, (i - 2) * 32)
                        v.scalar_tensor_tensor(out=yout[:, 1 - par, c], in0=ps_y[:, 1 - par, c], scalar=1.0 / WSCALE,
                                               in1=b2_cur[:, 1 - par], op0=ALU.mult,
                                               op1=ALU.add).then_inc(S2["ybias_done"], 1)
                if has(i + 1):
                    split_low(2)
                if has(i):
                    split(i, 2)
                if has(i + 1):
                    v.wait_ge(tile_ld[1 - par], ((i + 1) - (1 - par)) * 8 + 16)
                    came(v, "yout_done", i - 1, 2)
                    came(v, "act_done", i - 1, 4)
                    v.tensor_copy(b1_cur[:, 1 - par], b1T[:].rearrange("p e m -> p (e m)")[:, bass.ds(e * MF, MF)])
                    v.tensor_copy(gate_cur[:, 1 - par], tile_in[:, 1 - par, :, bass.ds(e + D, 1)].rearrange(
                        "p c w -> p (c w)")).then_inc(S2["prep_done"], 1)
                    split_low(3)
                if has(i):
                    split(i, 3)

            stage_two(v, step2)

        @block.tensor
        def _(pe):
            pe.wait_ge(const_in, 16)

            def step(n, par):
                if active(n, 1):
                    m = n - 1
                    reached(pe, "xn_done", m)
                    reached(pe, "xT_done", m - 1)
                    reached(pe, "xcol_done", m - 2)
                    if not is_int(n) or n - 6 >= 0:
                        reached(pe, "base_done", n - 6)
                    for b in range(B):
                        for k in range(KD):
                            last = pe.transpose(ps_xT[:, b, k], xn[:, 1 - par, b, k * P:(k + 1) * P], ident)
                    last.then_inc(S["xT_ps"], 1)
                if active(n, 4):
                    m = n - 4
                    reached(pe, "xm_done", m)
                    reached(pe, "logit_done", m - 1)
                    for b in range(B):
                        for k in range(KD):
                            last = pe.transpose(ps_mT[:, b, k], xm[:, par, b, k * P:(k + 1) * P], ident)
                    last.then_inc(S["mT_ps"], 1)
                if active(n, 3):
                    m, mp = n - 3, 1 - par
                    reached(pe, "read_done", m)
                    reached(pe, "readcol_done", m - 1)
                    reached(pe, "x1_done", m - 1)
                    for b in range(B):
                        for k in range(KD):
                            last = pe.matmul(ps_proj[:, b], readsT[:, mp, b, k, 0:P], wrT[:, k], start=(k == 0),
                                             stop=(k == KD - 1))
                    last.then_inc(S["proj_ps"], 1)
                if active(n, 2):
                    m = n - 2
                    reached(pe, "xT_done", m)
                    reached(pe, "xcol_done", m)
                    reached(pe, "score_done", m - 1)
                    for b in range(B):
                        for side in range(2):
                            d = slice(side * HD, (side + 1) * HD)
                            for k in range(KD):
                                last = pe.matmul(ps_score[:, side, b, k * P:(k + 1) * P], xnT[d, par, b, k, 0:P],
                                                 xnT[d, par, b, k, 1:P + 1], start=True, stop=True)
                    last.then_inc(S["score_ps"], 1)
                    reached(pe, "val_done", m - 1)
                    if is_int(m) and m == 0:
                        pe.wait_ge(proj_in, 32)
                    for b in range(B):
                        for k in range(KD):
                            last = pe.matmul(ps_val[:, b], xnT[:, par, b, k, 1:P + 1], wwT[:, k], start=(k == 0),
                                             stop=(k == KD - 1))
                    last.then_inc(S["val_ps"], 1)
                if active(n, 4):
                    m = n - 4
                    reached(pe, "mT_done", m)
                    if is_int(m) and m == 0:
                        pe.wait_ge(gate_in, 32)
                    for b in range(B):
                        for k in range(KD):
                            last = pe.matmul(ps_logit[:, b], xmT[:, b, k], gateT[:, k], start=(k == 0),
                                             stop=(k == KD - 1))
                    last.then_inc(S["logit_ps"], 1)
                if active(n, 5):
                    m = n - 5
                    reached(pe, "mask_done", m)
                    if is_int(m) and m == 0:
                        pe.wait_ge(setup_dve, 17)
                    if n - 1 < NCH if is_int(n) else True:
                        reached(pe, "xT_done", n - 1)
                    if (0 < n - 1 < NCH) if is_int(n) else True:
                        reached(pe, "xcol_done", n - 2)
                    pe.matmul(ps_rank, before16[:], mask[:], start=True, stop=True)
                    pe.matmul(ps_rank[:, 1], ones16[:], mask[:, 0], start=False, stop=True, skip_group_check=True)
                    pe.matmul(ps_total, ones16[:], mask[:, 0], start=True, stop=False)
                    pe.matmul(ps_total, ones16[:], mask[:, 1], start=False, stop=True).then_inc(S["rank_ps"], 1)
                if active(n, 2):
                    m = n - 2
                    reached(pe, "keys_done", m)
                    reached(pe, "val_done", m)
                    reached(pe, "state_done", m - 1)
                    for b in range(B):
                        for k in range(KD):
                            last = pe.matmul(ps_state[:, b, k], keys[:, par, b, k * P:(k + 1) * P],
                                             vals[:, b, k * P:(k + 1) * P], start=True, stop=True)
                    last.then_inc(S["state_ps"], 1)
                    reached(pe, "queries_done", m)
                    if is_int(m) and m == 0:
                        pe.wait_ge(setup_pool, 2)
                    reached(pe, "score_done", m)
                    reached(pe, "read_done", m - 1)
                    reached(pe, "readcol_done", m - 1)
                    for b in range(B):
                        for k in range(KD):
                            pe.matmul(ps_read[:, b, k], state[:, b, k], queries[:, b, k], start=True, stop=True)
                            for side in range(2):
                                h = 2 * k + side
                                last = pe.matmul(ps_read[side * HD:(side + 1) * HD, b, k],
                                                 vals[:, b, h * HD:(h + 1) * HD], scores[:, b, side, k],
                                                 start=False, stop=True, skip_group_check=True)
                    last.then_inc(S["read_ps"], 1)

            stage_one(pe, step)

            pe.wait_ge(table_done, 1)
            w1_of = lambda par, k, lo, m: wcur[:, par, k * 2 * PIECE + lo * PIECE + m * P:][:, 0:P]
            w2_of = lambda par, m, lo: wcur[:, par, (2 + m // 4) * 2 * PIECE + lo * PIECE + (m % 4) * D:][:, 0:D]

            def first(i, par, pair):
                s = pair % 2
                if pair == 0:
                    came(pe, "wcur_done", i, 4, 1)
                    came(pe, "tileT_done", i)
                if pair >= 2:
                    came(pe, "act_done", i, 4, pair - 2)
                else:
                    came(pe, "act_done", i - 1, 4, pair + 2)
                for mm in range(2):
                    m = 2 * pair + mm
                    n = 0
                    for k in range(KD):
                        for lo, part in ((0, k), (0, KD + k), (1, k)):
                            last = pe.matmul(ps_h[:, s, mm], w1_of(par, k, lo, m), tileT[:, par, part],
                                             start=(n == 0), stop=(n == 3 * KD - 1))
                            n += 1
                last.then_inc(S2["h_ps"], 1)

            def second(i, par, pair):
                s = pair
                came(pe, "split_done", i, 4, pair)
                if pair % 2 == 0:
                    came(pe, "wcur_done", i, 4, 2 + pair // 2)
                if pair == 0:
                    came(pe, "ybias_done", i - 2, 2)
                for mm in range(2):
                    m = 2 * pair + mm
                    for c in range(2):
                        hh = h_hi[:, s, mm, c * P:(c + 1) * P]
                        hl = h_lo[:, s, mm, c * P:(c + 1) * P]
                        for n, (lhs, lo) in enumerate(((hh, 0), (hh, 1), (hl, 0))):
                            last = pe.matmul(ps_y[:, par, c], lhs, w2_of(par, m, lo), start=(m == 0 and n == 0),
                                             stop=(m == MF - 1 and n == 2))
                last.then_inc(S2["l2_done"], 1)

            def step2(i, par):
                if has(i):
                    first(i, par, 0)
                if has(i - 1):
                    second(i - 1, 1 - par, 2)
                if has(i):
                    first(i, par, 1)
                if has(i - 1):
                    second(i - 1, 1 - par, 3)
                if has(i + 1):
                    pe.wait_ge(tile_ld[1 - par], ((i + 1) - (1 - par)) * 8 + 16)
                    came(pe, "tileT_done", i)
                    for part in range(4):
                        for c in range(2):
                            words = tile_in[:, 1 - par, c, 0:D].bitcast(F16)
                            last = pe.transpose(ps_tileT[:, part, c * P:(c + 1) * P],
                                                words[:, part * P:(part + 1) * P], ident16[:])
                    last.then_inc(S2["tileT_ps"], 1)
                if has(i):
                    first(i, par, 2)
                    second(i, par, 0)
                    first(i, par, 3)
                    second(i, par, 1)

            stage_two(pe, step2)


def kernel(L0_attn_out, L0_attn_W_write, L0_attn_W_read, L0_attn_decay, L0_attn_log_alpha,
           L0_ffn_gate_w, L0_ffn_w1, L0_ffn_b1, L0_ffn_w2, L0_ffn_b2):
    import concourse.bacc as bacc
    from concourse.bass_utils import run_bass_kernel_spmd

    blocks = lambda w: np.ascontiguousarray(w.reshape(KD, P, -1).transpose(1, 0, 2))
    w1 = np.asarray(L0_ffn_w1).transpose(1, 2, 0).reshape(E, KD, P, F)
    w2 = np.asarray(L0_ffn_w2).transpose(1, 2, 0).reshape(E, 2, 4, P, D)
    w2 = w2.transpose(0, 1, 3, 2, 4).reshape(E, 2, P, 4 * D)
    arrays = {
        "x": np.ascontiguousarray(L0_attn_out),
        "w_write": blocks(np.asarray(L0_attn_W_write).T),
        "w_read": blocks(np.asarray(L0_attn_W_read).T),
        "decay": np.ascontiguousarray(L0_attn_decay),
        "log_alpha": np.ascontiguousarray(L0_attn_log_alpha),
        "gate_w": blocks(np.asarray(L0_ffn_gate_w).T),
        "experts": np.ascontiguousarray(np.concatenate([w1, w2], axis=1).reshape(NPIECE, P, PIECE)),
        "b1": np.ascontiguousarray(np.asarray(L0_ffn_b1).reshape(E, MF, P).transpose(2, 0, 1)),
        "b2": np.ascontiguousarray(L0_ffn_b2),
        "const": constants(),
    }
    nc = bacc.Bacc("TRN2", target_bir_lowering=False, num_devices=1)
    args = [nc.dram_tensor(f"in_{n}", v.shape, mybir.dt.from_np(v.dtype), kind="ExternalInput").ap()
            for n, v in arrays.items()]
    out = nc.dram_tensor("out", (TOK + TILE, D), F32, kind="ExternalOutput").ap()
    build(nc, *args, out)
    r = run_bass_kernel_spmd(nc, [{f"in_{n}": v for n, v in arrays.items()}], core_ids=[0])
    return np.asarray(r.results[0]["out"])[:TOK].reshape(B, T, D)
```

```python
from contextlib import ExitStack

import numpy as np

import concourse.bass as bass
from concourse import mybir

F32 = mybir.dt.float32
F16 = mybir.dt.float16
BF16 = mybir.dt.bfloat16
I32 = mybir.dt.int32
U32 = mybir.dt.uint32
ALU = mybir.AluOpType
ACT = mybir.ActivationFunctionType
AX = mybir.AxisListType

P = 128
B, T, D = 2, 2048, 256
H, HD = 4, 64
E, F = 8, 1024
KD = D // P
MF = F // P
NCH = T // P
TOK = B * T
EPS = 1e-5
TILE = 256
CAP = TILE + TOK
NT = (2 * TOK + E * (TILE - 1)) // TILE
ROW = D + E + 1
WSCALE = 64.0
PIECE = 1024
NPIECE = E * 4
EW = 4 * PIECE
HIGH_LOW = ((0, 0), (0, 1), (1, 0))
LAG = 5
PEEL1 = LAG + 2

CONST = {}
_at = 0
for _name, _width in (("ident", P), ("before", P), ("gap", P), ("index", P), ("left", 1), ("experts", E),
                      ("region", E), ("token", 2 * NCH), ("padtoken", 2), ("place", 2), ("step", TOK // TILE),
                      ("upto", E * E), ("tile", NT)):
    CONST[_name] = (_at, _width)
    _at += _width
NCONST = _at


def constants():
    c = np.zeros((P, NCONST), np.float32)
    p = np.arange(P)[:, None]
    f = np.arange(P)[None, :]

    def put(name, value):
        a, w = CONST[name]
        c[:, a:a + w] = value

    put("ident", p == f)
    put("before", p < f)
    put("gap", np.maximum(f - 1 - p, 0))
    put("index", f)
    put("left", P - 1 - p)
    put("experts", np.arange(E)[None, :])
    put("region", np.arange(E)[None, :] * CAP + TILE)
    q = np.arange(2 * NCH)[None, :]
    put("token", (q % 2) * T + (q // 2) * P + p)
    put("padtoken", TOK + 2 * p + np.arange(2)[None, :])
    put("place", P * np.arange(2)[None, :] + p)
    put("step", np.arange(TOK // TILE)[None, :] * TILE)
    put("upto", (np.arange(E)[None, :] <= np.arange(E)[:, None]).reshape(1, -1))
    put("tile", np.arange(NT)[None, :])
    return c


def build(nc, x, w_write, w_read, decay, log_alpha, gate_w, experts, b1, b2, const, out):
    with ExitStack() as ctx:
        def sb(name, shape, dt=F32):
            return ctx.enter_context(nc.sbuf_tensor(name, shape, dt))

        def sem(name):
            return ctx.enter_context(nc.semaphore(name))

        sent = nc.dram_tensor("sent_rows", (E * CAP, ROW), F32, kind="Internal").ap()
        sent16 = sent.bitcast(F16)
        x_rows = x.rearrange("b t d -> (b t) d")

        weights = sb("weights", [P, E * EW])
        consts = sb("consts", [P, NCONST])

        def const_of(name, rows=P):
            a, w = CONST[name]
            return consts[0:rows, a:a + w]

        ident = const_of("ident")
        before = const_of("before")
        ident16 = sb("ident16", [P, P], F16)
        before16 = sb("before16", [P, P], BF16)
        ones16 = sb("ones16", [P, P], BF16)
        proj16 = sb("proj16", [P, 2, 2, KD * D], F16)
        wwT16 = proj16[:, :, 0].rearrange("p h (k d) -> p h k d", k=KD)
        wrT16 = proj16[:, :, 1].rearrange("p h (k d) -> p h k d", k=KD)
        gateT = sb("gateT", [P, KD, E])
        gam = sb("gam", [P, H])
        lng = sb("lng", [P, H + KD])
        alphas = sb("alphas", [P, H + KD])
        decayM = sb("decayM", [P, 2, KD, P])
        decayQ = sb("decayQ", [P, KD, P])
        decayK = sb("decayK", [P, H])
        decayC = sb("decayC", [P, KD])
        b1T = sb("b1T", [P, E, MF])
        minus_half = sb("minus_half", [P, 1])
        warm = sb("warm", [P, 1])
        zcol = sb("zcol", [P, B * KD, 1])
        base = sb("base", [P, E])
        token_i = sb("token_i", [P, 2 * NCH], I32)
        pad = sb("pad", [P, 2, ROW])
        tab = sb("tab", [P, 3 * E + 8 * NT])
        cmp = sb("cmp", [P, max(E * TOK // TILE, NT * E)])
        cmp2 = sb("cmp2", [P, NT * E])
        tab_i = sb("tab_i", [P, 2 * NT], I32)
        tile_row_i = tab_i[:, 0:NT]
        tile_exp_i = tab_i[:, NT:2 * NT]

        ARENA = 14912
        arena = sb("arena", [P, ARENA])
        at = [0]

        def carve(words):
            a = at[0]
            at[0] += words
            assert at[0] <= ARENA, at[0]
            return arena[:, a:a + words]

        res = carve(4 * 2 * D)
        xt = carve(2 * 2 * D).rearrange("p (s b d) -> p s b d", s=2, b=2)
        xn = carve(2 * 2 * D).rearrange("p (s b d) -> p s b d", s=2, b=2)
        xnT = carve(2 * 2 * KD * (P + 1)).bitcast(F16).rearrange("p (h s b k t) -> p h s b k t", h=2, s=2, b=2, k=KD)
        keys = carve(2 * 2 * D).rearrange("p (s b d) -> p s b d", s=2, b=2)
        queries = carve(2 * 2 * D).rearrange("p (s b k t) -> p s b k t", s=2, b=2, k=KD)
        vals = carve(2 * D).rearrange("p (b d) -> p b d", b=2)
        scores = carve(2 * H * P).rearrange("p (b s k t) -> p b s k t", b=2, s=2, k=KD)
        readsT = carve(2 * 2 * KD * (P + 1)).bitcast(F16).rearrange("p (h s b k t) -> p h s b k t", h=2, s=2, b=2,
                                                                    k=KD)
        xm = carve(2 * 2 * D).rearrange("p (s b d) -> p s b d", s=2, b=2)
        xmT = carve(2 * D).rearrange("p (b k t) -> p b k t", b=2, k=KD)
        row_words = carve(2 * 2 * ROW)
        row = row_words.rearrange("p (s b w) -> p s b w", s=2, b=2)
        proj_words = row_words[:, 0:2 * KD * D].rearrange("p (w c) -> p w c", w=2)
        state = carve(2 * D).rearrange("p (b k i) -> p b k i", b=2, k=KD)
        faded = carve(2 * D).rearrange("p (b k i) -> p b k i", b=2, k=KD)
        end_one = at[0]
        at[0] = 0
        tileT = carve(2 * 4 * TILE // 2).bitcast(F16).rearrange("p (s k t) -> p s k t", s=2, k=4)
        wcur = carve(2 * EW).bitcast(F16).rearrange("p (s w) -> p s w", s=2)
        tile_in = carve(2 * 2 * (E + 1)).rearrange("p (s c w) -> p s c w", s=2, c=2)
        act = carve(2 * 2 * TILE).rearrange("p (s w) -> p s w", s=2)
        h_hi = carve(4 * TILE).bitcast(F16).rearrange("p (s m t) -> p s m t", s=4, m=2)
        h_lo = carve(4 * TILE).bitcast(F16).rearrange("p (s m t) -> p s m t", s=4, m=2)
        yout = carve(2 * 2 * D).rearrange("p (s c d) -> p s c d", s=2, c=2)
        b1_cur = carve(2 * MF).rearrange("p (s m) -> p s m", s=2)
        b2_cur = carve(2 * D).rearrange("p (s d) -> p s d", s=2)
        gate_cur = carve(4).rearrange("p (s c) -> p s c", s=2)
        tok_cur = carve(4).bitcast(I32).rearrange("p (s c) -> p s c", s=2)
        zrow = arena[:, end_one:end_one + 2 * D]
        assert end_one + 2 * D <= ARENA

        small_at = [0]
        tiny = sb("tiny", [P, 176])

        def small(w, dt=F32):
            a = small_at[0]
            small_at[0] += w
            v = tiny[:, a:a + w]
            return v if dt == F32 else v.bitcast(dt)

        by_batch = lambda v: v.rearrange("p (b e) -> p b e", b=B)
        stats1 = by_batch(small(B * 6))
        moments1 = by_batch(small(B * 2))
        ve1, rs1 = small(B), small(B)
        stats2 = by_batch(small(B * 6))
        moments2 = by_batch(small(B * 2))
        ve2, rs2 = small(B), small(B)
        logit = by_batch(small(B * E))
        top = by_batch(small(B * 8))
        top_at = by_batch(small(B * 8, U32))
        shifted = by_batch(small(B * E))
        masked = by_batch(small(B * E))
        esum, rsum = small(B), small(B)
        slot_i = small(2 * B * 2, I32).rearrange("p (s w) -> p s w", s=2)
        slots = by_batch(small(B * E))
        assert small_at[0] <= 176
        pick = sb("pick", [P, B, 2, E])
        picked = sb("picked", [P, B, 2, E])
        mask = sb("mask", [P, B, E], BF16)

        psum = ctx.enter_context(nc.psum_tensor("psum", [P, 8, 512], F32))
        ps_xT = psum[:, 0, :].rearrange("p (b k t) -> p b k t", b=2, k=KD)
        ps_mT = psum[:, 1, :].rearrange("p (b k t) -> p b k t", b=2, k=KD)
        ps_rank = psum[:, 7, 0:B * E].rearrange("p (b e) -> p b e", b=B)
        ps_total = psum[:, 7, B * E:B * E + E]
        ps_logit = psum[:, 1, 0:B * E].rearrange("p (b e) -> p b e", b=B)
        ps_val = psum[:, 2, :].rearrange("p (b d) -> p b d", b=2)
        ps_score = psum[:, 3:5, :].rearrange("p s (b w) -> p s b w", b=2)
        ps_read = psum[:, 5, :].rearrange("p (b k t) -> p b k t", b=2, k=KD)
        ps_state = psum[:, 6, :].rearrange("p (b k i) -> p b k i", b=2, k=KD)
        ps_proj = psum[:, 7, :].rearrange("p (b d) -> p b d", b=2)
        ps_h = psum[:, 0:2, :].rearrange("p s (m t) -> p s m t", m=2)
        ps_y = psum[:, 4:8, 0:D].rearrange("p (s c) d -> p s c d", s=2)

        const_in = sem("const_in")
        decay_in = sem("decay_in")
        proj_in = sem("proj_in")
        gate_in = sem("gate_in")
        setup_act = sem("setup_act")
        setup_dve = sem("setup_dve")
        setup_pool = sem("setup_pool")
        x_in = [sem(f"x_in{s}") for s in range(2)]
        w_in = sem("w_in")
        row_out = [sem(f"row_out{s}") for s in range(2)]
        x1_out = [sem(f"x1_out{s}") for s in range(2)]
        zrow_out = sem("zrow_out")
        S = {n: sem(n) for n in (
            "stats1_done", "moments1_done", "ve1_done", "rs1_done", "xn_done", "xT_ps", "xT_done", "xcol_done", "xlo_done",
            "res_done", "keys_done", "queries_done", "val_ps", "val_done", "score_ps", "score_done",
            "read_ps", "read_done", "readlo_done", "state_ps", "state_done", "faded_done", "proj_ps",
            "x1_done", "stats2_done", "moments2_done", "ve2_done", "rs2_done", "xm_done", "hi_done", "lo_done",
            "mT_ps", "mT_done", "logit_ps", "logit_done", "top_done", "top_at_done", "shifted_done", "exp_done",
            "pick_done", "mask_done", "esum_done", "rsum_done", "masked_done", "rank_ps", "slots_done",
            "picked_done", "slot_i_done", "base_done", "gates_done", "token_done")}
        carrier = [sem("carrier_dve"), sem("carrier_pool")]
        table_done = sem("table_done")
        buffers_free = sem("buffers_free")
        table_step = sem("table_step")
        pad_out = sem("pad_out")
        b2_in = [sem(f"b2_in{s}") for s in range(2)]
        tile_ld = [sem(f"tile_ld{s}") for s in range(2)]
        tileT_ld = [sem(f"tileT_ld{s}") for s in range(2)]
        S2 = {n: sem(n) for n in ("tileT_used", "prep_done", "whi_done", "wcur_done", "tok_done", "h_ps", "act_done",
                                  "hhi_done", "split_done", "l2_done", "ybias_done", "yout_done")}
        added = sem("added")

        block = ctx.enter_context(nc.Block())

        def is_int(n):
            return isinstance(n, int)

        def active(n, lag):
            return not is_int(n) or 0 <= n - lag < NCH

        def reached(eng, name, n):
            if not is_int(n) or n >= 0:
                eng.wait_ge(S[name], n + 1)

        def plainly(eng, *waits):
            for s, v in waits:
                if not is_int(v) or v > 0:
                    eng.wait_ge(s, v)
            if any(not is_int(v) for s, v in waits):
                eng.sem_inc(carrier[eng is nc.gpsimd], 1)

        def loaded(eng, slot_sem, n, par, each=16):
            if not is_int(n) or n >= 0:
                eng.wait_ge(slot_sem, (n - par) * (each // 2) + each)

        def stage_one(eng, step):
            for n in range(PEEL1):
                step(n, n % 2)
            trips = (NCH - 1 - PEEL1) // 2
            with eng.Fori(0, trips) as j:
                step(2 * j + PEEL1, PEEL1 % 2)
                step(2 * j + PEEL1 + 1, (PEEL1 + 1) % 2)
            for n in range(PEEL1 + 2 * trips, NCH + LAG + 1):
                step(n, n % 2)

        def stored(eng):
            for s in range(2):
                eng.wait_ge(x1_out[s], 16 * NCH // 2)
            eng.wait_ge(zrow_out, 16)

        def res_of(n):
            a = (n % 4) * (B * D)
            v = res[:, a:a + B * D] if is_int(a) else res[:, bass.ds(a, B * D)]
            return v.rearrange("p (b d) -> p b d", b=B)

        def both(rows, n):
            v = rows[0:B * T, :].rearrange("(b t) d -> t b d", b=B)
            return v[n * P:(n + 1) * P] if is_int(n) else v[bass.ds(n * P, P)]

        def stage_two(eng, step):
            step(-1, 1)
            step(0, 0)
            step(1, 1)
            trips = (NT - 4) // 2
            with eng.Fori(0, trips) as j:
                step(2 * j + 2, 0)
                step(2 * j + 3, 1)
            for i in range(2 + 2 * trips, NT + 1):
                step(i, i % 2)

        def has(i):
            return not is_int(i) or 0 <= i < NT

        def came(eng, name, i, per=1, k=None):
            if not is_int(i) or i >= 0:
                eng.wait_ge(S2[name], i * per + (per if k is None else k + 1))

        @block.sync
        def _(sp):
            def load_x(n, par):
                reached(sp, "res_done", n - 2)
                reached(sp, "xn_done", n - 2)
                sp.dma_start(xt[:, par], both(x_rows, n)).then_inc(x_in[par], 16)

            for src, dst in ((decay, gam), (log_alpha, alphas)):
                sp.dma_start(dst[:, 0:H], src.rearrange("(a h) -> a h", a=1).to_broadcast([P, H])).then_inc(decay_in, 16)
            load_x(0, 0)
            sp.dma_start(consts[:], const).then_inc(const_in, 16)
            load_x(1, 1)
            for i, src in enumerate((w_write, w_read)):
                sp.dma_start(proj_words[:, i], src.rearrange("p k d -> p (k d)")).then_inc(proj_in, 16)
            sp.dma_start(gateT[:], gate_w).then_inc(gate_in, 16)
            sp.dma_start(b1T[:], b1).then_inc(gate_in, 16)

            def step(n, par):
                if (active(n + 1, 0) and n > 0) if is_int(n) else True:
                    load_x(n + 1, 1 - par)
                if active(n, 0):
                    src = experts[2 * n:2 * n + 2] if is_int(n) else experts[bass.ds(2 * n, 2)]
                    o = 2 * n * PIECE
                    dst = weights[:, o:o + 2 * PIECE] if is_int(n) else weights[:, bass.ds(o, 2 * PIECE)]
                    sp.dma_start(dst.rearrange("p (a w) -> p a w", a=2),
                                 src.rearrange("a p w -> p a w")).then_inc(w_in, 16)
                if is_int(n) and n in (4, 5):
                    sp.wait_ge(setup_dve, 18)
                    for e in range((n - 4) * E // 2, (n - 3) * E // 2):
                        sp.dma_start(sent[e * CAP:e * CAP + TILE, :].rearrange("(p c) w -> p (c w)", c=2),
                                     pad[:].rearrange("p c w -> p (c w)")).then_inc(pad_out, 16)
                    if n == 5:
                        sp.wait_ge(setup_pool, 3)
                        sp.dma_start(out[TOK:TOK + TILE, :].rearrange("(p c) d -> p (c d)", c=2),
                                     zrow).then_inc(zrow_out, 16)
                if active(n, 3):
                    m = n - 3
                    reached(sp, "x1_done", m)
                    if active(n, 1):
                        reached(sp, "res_done", m + 2)
                    sp.dma_start(both(out, m), res_of(m)).then_inc(x1_out[1 - par], 16)

            stage_one(sp, step)

            sp.wait_ge(table_done, 1)
            r0 = sp.value_load(tile_row_i[0:1, 0:1], min_val=0, max_val=E * CAP - TILE)
            for s in range(2):
                sp.wait_ge(row_out[s], 64 * NCH // 2)
            reached(sp, "gates_done", NCH - 1)
            stored(sp)
            sp.wait_ge(pad_out, 16 * E)

            def load_tile(i, par):
                came(sp, "tileT_used", i - 2)
                came(sp, "prep_done", i - 2)
                came(sp, "tok_done", i - 2)
                at_i = tile_row_i[0:1, i:i + 1] if is_int(i) else tile_row_i[0:1, bass.ds(i, 1)]
                r = r0 if is_int(i) and i == 0 else sp.value_load(at_i, min_val=0, max_val=E * CAP - TILE)
                sp.dma_start_transpose(tileT[:, par], sent16[bass.ds(r, TILE), 0:2 * D]).then_inc(tileT_ld[par], 16)
                sp.dma_start(tile_in[:, par],
                             sent[bass.ds(r, TILE), D:ROW].rearrange("(c p) w -> p c w", c=2)).then_inc(tile_ld[par], 16)
                came(sp, "ybias_done", i - 2, 2)
                at_i = tile_exp_i[0:1, i:i + 1] if is_int(i) else tile_exp_i[0:1, bass.ds(i, 1)]
                e = sp.value_load(at_i, min_val=0, max_val=E - 1)
                sp.dma_start(b2_cur[:, par], b2[bass.ds(e, 1), :].to_broadcast([P, D])).then_inc(b2_in[par], 16)

            def step2(i, par):
                if has(i + 1):
                    load_tile(i + 1, 1 - par)

            stage_two(sp, step2)

        @block.gpsimd
        def _(pool):
            pool.memset(minus_half[:], -0.5).then_inc(setup_pool, 1)
            pool.memset(zcol[:], 0.0)
            pool.memset(state[:], 0.0)
            for part in range(2):
                last = pool.memset(readsT[:, part, 0, :, :, 0:1], 0.0)
            last.then_inc(setup_pool, 1)
            pool.memset(zrow, 0.0).then_inc(setup_pool, 1)
            pool.memset(pad[:], 0.0).then_inc(setup_pool, 1)
            pool.wait_ge(setup_pool, 1)

            def step(n, par):
                for lag, moments, ve, rs, got, mid, end, used in (
                        (0, moments1, ve1, rs1, "moments1_done", "ve1_done", "rs1_done", "xn_done"),
                        (3, moments2, ve2, rs2, "moments2_done", "ve2_done", "rs2_done", "xm_done")):
                    if active(n, lag):
                        m = n - lag
                        plainly(pool, (S[got], m + 1))
                        pool.tensor_scalar(ve, moments[:, :, 1], EPS, None, ALU.add).then_inc(S[mid], 1)
                        reached(pool, mid, m)
                        reached(pool, used, m - 1)
                        pool.tensor_tensor(rs, ve, minus_half[:].to_broadcast([P, B]), ALU.pow).then_inc(S[end], 1)
                if active(n, 0):
                    reached(pool, "xn_done", n)
                    loaded(pool, x_in[par], n, par)
                    loaded(pool, x1_out[par], n - 4, par)
                    pool.tensor_tensor(res_of(n), xt[:, par], xn[:, par], ALU.add).then_inc(S["res_done"], 1)
                if active(n, 5):
                    m, mp = n - 5, 1 - par
                    if is_int(m) and m == 0:
                        pool.wait_ge(setup_dve, 18)
                    if is_int(m) and m > NCH - 5:
                        loaded(pool, row_out[mp], m - 2, mp, 64)
                    src = token_i[:, 2 * m:2 * m + 2] if is_int(m) else token_i[:, bass.ds(2 * m, 2)]
                    pool.tensor_copy(row[:, mp, :, ROW - 1].bitcast(I32), src).then_inc(S["token_done"], 1)
                    plainly(pool, *((S[name], m + 1) for name in
                                    ("token_done", "lo_done", "hi_done", "gates_done", "slot_i_done")))
                    for b in range(B):
                        for k in range(2):
                            at_bk = slot_i[:, mp, 2 * b + k:2 * b + k + 1]
                            pool.indirect_dma_start(
                                out=sent, out_offset=bass.IndirectOffsetOnAxis(ap=at_bk, axis=0),
                                in_=row[:, mp, b, :], in_offset=None).then_inc(row_out[mp], 16)
                if active(n, 4) and not (is_int(n) and n > NCH):
                    m = n - 4
                    reached(pool, "hi_done", m)
                    words = row[:, par, :, 0:D].bitcast(F16)
                    pool.tensor_tensor(words[:, :, D:2 * D], xm[:, par], words[:, :, 0:D],
                                       ALU.subtract).then_inc(S["lo_done"], 1)

            stage_one(pool, step)

            stored(pool)

            def step2(i, par):
                if is_int(i) and i == -1:
                    copy_tokens(0, 0)
                if has(i - 1):
                    for c in range(2):
                        plainly(pool, (S2["yout_done"], (i - 1) * 2 + c + 1), (S2["tok_done"], i),
                                (added, (i - 1) * 32))
                        pool.indirect_dma_start(
                            out=out, out_offset=bass.IndirectOffsetOnAxis(ap=tok_cur[:, 1 - par, c:c + 1], axis=0),
                            in_=yout[:, 1 - par, c], in_offset=None, compute_op=ALU.add).then_inc(added, 16)
                if has(i) and has(i + 1):
                    copy_tokens(i + 1, 1 - par)

            def copy_tokens(i, par):
                plainly(pool, (tile_ld[par], (i - par) * 8 + 16), (added, (i - 1) * 32))
                pool.tensor_copy(tok_cur[:, par], tile_in[:, par, :, E].bitcast(I32)).then_inc(S2["tok_done"], 1)

            stage_two(pool, step2)
            pool.wait_ge(added, 32 * NT)

        @block.scalar
        def _(a):
            a.wait_ge(decay_in, 32)
            a.activation(gam[:], gam[:], ACT.Exp, scale=-1.0).then_inc(setup_act, 1)
            a.wait_ge(setup_dve, 2)
            a.activation(lng[:, 0:H], gam[:], ACT.Ln).then_inc(setup_act, 1)
            a.wait_ge(setup_act, 2)
            a.wait_ge(const_in, 16)
            for h in range(H):
                a.activation(decayM[:, h % 2, h // 2, :], const_of("gap"), ACT.Exp, scale=lng[:, h:h + 1],
                             bias=alphas[:, h:h + 1])
            a.activation(decayK[:], lng[:, 0:H], ACT.Exp, scale=const_of("left")).then_inc(setup_act, 1)
            a.wait_ge(setup_dve, 6)
            for k in range(KD):
                a.activation(decayQ[:, k, :], const_of("index"), ACT.Exp, scale=lng[:, H + k:H + k + 1],
                             bias=alphas[:, H + k:H + k + 1]).then_inc(setup_act, 1)
            a.activation(decayC[:], lng[:, H:H + KD], ACT.Exp, scale=float(P)).then_inc(setup_act, 1)
            a.wait_ge(setup_act, 6)

            def step(n, par):
                if active(n, 1):
                    m = n - 1
                    reached(a, "xT_ps", m)
                    reached(a, "score_ps", m - 2)
                    reached(a, "val_ps", m - 2)
                    a.activation(xnT[:, 0, 1 - par, :, :, 0:P].rearrange("p b k t -> p (b k) t"),
                                 ps_xT.rearrange("p b k t -> p (b k) t"), ACT.Copy).then_inc(S["xT_done"], 1)
                if (0 < n - 1 <= NCH) if is_int(n) else True:
                    ended = is_int(n) and n - 1 == NCH
                    reached(a, "read_ps", n - 4)
                    for k in range(KD):
                        src = zcol[:, 0:B] if ended else ps_xT[:, :, k, 0:1]
                        a.activation(queries[:, par, :, k, P - 1:P], src, ACT.Copy, scale=decayQ[:, k, P - 1:P])
                    src = zcol[:] if ended else ps_xT[:, :, :, 0:1].rearrange("p b k t -> p (b k) t")
                    a.activation(xnT[:, 0, par, :, :, P:P + 1].rearrange("p b k t -> p (b k) t"), src,
                                 ACT.Copy).then_inc(S["xcol_done"], 1)
                if is_int(n) and n == 1:
                    a.wait_ge(proj_in, 32)
                    a.activation(proj16[:, 0].rearrange("p w c -> p (w c)"), proj_words.rearrange("p w c -> p (w c)"),
                                 ACT.Copy, scale=WSCALE).then_inc(setup_act, 1)
                if active(n, 4):
                    m = n - 4
                    reached(a, "mT_ps", m)
                    reached(a, "logit_ps", m - 1)
                    a.activation(xmT.rearrange("p b k t -> p (b k t)"), ps_mT.rearrange("p b k t -> p (b k t)"),
                                 ACT.Copy).then_inc(S["mT_done"], 1)
                if active(n, 1):
                    m = n - 1
                    reached(a, "xn_done", m)
                    reached(a, "state_ps", m - 2)
                    for h in range(H):
                        d = slice(h * HD, (h + 1) * HD)
                        last = a.activation(keys[:, 1 - par, :, d], xn[:, 1 - par, :, d], ACT.Copy,
                                            scale=decayK[:, h:h + 1])
                    last.then_inc(S["keys_done"], 1)
                if active(n, 2):
                    m = n - 2
                    reached(a, "state_done", m - 1)
                    if is_int(m) and m == 0:
                        a.wait_ge(setup_pool, 2)
                    for k in range(KD):
                        last = a.activation(faded[:, :, k], state[:, :, k], ACT.Copy, scale=decayC[:, k:k + 1])
                    last.then_inc(S["faded_done"], 1)
                if active(n, 2):
                    m = n - 2
                    reached(a, "val_ps", m)
                    reached(a, "state_ps", m - 1)
                    reached(a, "read_ps", m - 1)
                    a.activation(vals, ps_val, ACT.Copy, scale=1.0 / WSCALE).then_inc(S["val_done"], 1)
                if active(n, 5):
                    m = n - 5
                    reached(a, "shifted_done", m)
                    a.activation(shifted, shifted, ACT.Exp).then_inc(S["exp_done"], 1)
                if active(n, 4):
                    m = n - 4
                    reached(a, "xm_done", m)
                    if is_int(m) and m == 0:
                        a.wait_ge(setup_dve, 14)
                    loaded(a, row_out[par], m - 2, par, 64)
                    a.activation(row[:, par, :, 0:D].bitcast(F16)[:, :, 0:D], xm[:, par],
                                 ACT.Copy).then_inc(S["hi_done"], 1)
                if active(n, 2):
                    m = n - 2
                    reached(a, "read_ps", m)
                    reached(a, "proj_ps", m - 1)
                    reached(a, "readlo_done", m - 1)
                    a.activation(readsT[:, 0, par, :, :, 1:P + 1].rearrange("p b k t -> p (b k) t"),
                                 ps_read.rearrange("p b k t -> p (b k) t"), ACT.Copy)
                    a.activation(readsT[:, 0, 1 - par, :, :, 0:1].rearrange("p b k t -> p (b k) t"),
                                 ps_read[:, :, :, P - 1:P].rearrange("p b k t -> p (b k) t"),
                                 ACT.Copy).then_inc(S["read_done"], 1)

            stage_one(a, step)

            a.wait_ge(table_done, 1)

            def gelu(i, par, pair):
                s = pair % 2
                came(a, "h_ps", i, 4, pair)
                if pair == 3:
                    a.sem_inc(S2["tileT_used"], 1)
                if pair == 0:
                    came(a, "prep_done", i)
                if pair >= 2:
                    came(a, "split_done", i, 4, pair - 2)
                else:
                    came(a, "split_done", i - 1, 4, pair + 2)
                for m in range(2):
                    mm = 2 * pair + m
                    last = a.activation(act[:, s, m * TILE:(m + 1) * TILE], ps_h[:, s, m], ACT.Gelu_apprx_tanh,
                                        scale=1.0 / WSCALE, bias=b1_cur[:, par, mm:mm + 1])
                last.then_inc(S2["act_done"], 1)

            def step2(i, par):
                if has(i + 1):
                    at_i = tile_exp_i[0:1, i + 1:i + 2] if is_int(i) else tile_exp_i[0:1, bass.ds(i + 1, 1)]
                    e = a.value_load(at_i, min_val=0, max_val=E - 1)
                    if is_int(i) and i == -1:
                        a.wait_ge(buffers_free, 1)

                def split_high(part):
                    if part == 0:
                        came(a, "h_ps", i - 1, 4)
                        if is_int(i) and i == -1:
                            a.wait_ge(w_in, 16 * NCH)
                    if part == 2:
                        came(a, "l2_done", i - 1, 4)
                    w = 2 * part * PIECE
                    a.activation(wcur[:, 1 - par, w:w + PIECE], weights[:, bass.ds(e * EW + part * PIECE, PIECE)],
                                 ACT.Copy, scale=WSCALE).then_inc(S2["whi_done"], 1)

                if has(i + 1):
                    split_high(0)
                if has(i):
                    gelu(i, par, 0)
                if has(i + 1):
                    split_high(1)
                if has(i):
                    gelu(i, par, 1)
                if has(i + 1):
                    split_high(2)
                if has(i):
                    gelu(i, par, 2)
                if has(i - 1):
                    for c in range(2):
                        came(a, "ybias_done", i - 1, 2, c)
                        a.activation(yout[:, 1 - par, c], yout[:, 1 - par, c], ACT.Copy,
                                     scale=gate_cur[:, 1 - par, c:c + 1]).then_inc(S2["yout_done"], 1)
                if has(i + 1):
                    if is_int(i) and i == -1:
                        a.activation(warm[:], minus_half[:], ACT.Gelu_apprx_tanh)
                    split_high(3)
                if has(i):
                    gelu(i, par, 3)

            stage_two(a, step2)

        @block.vector
        def _(v):
            v.wait_ge(setup_act, 1)
            v.tensor_scalar(gam[:], gam[:], 1.0, None, ALU.add).then_inc(setup_dve, 1)
            v.wait_ge(setup_dve, 1)
            v.reciprocal(gam[:], gam[:]).then_inc(setup_dve, 1)
            for got, table in ((1, alphas), (2, lng)):
                v.wait_ge(setup_act, got)
                for side in range(2):
                    rows = slice(side * HD, (side + 1) * HD)
                    v.tensor_copy(table[rows, H:H + KD],
                                  table[rows, 0:H].rearrange("p (k s) -> p k s", s=2)[:, :, side]).then_inc(setup_dve, 1)
            v.memset(ones16[:], 1.0).then_inc(setup_dve, 1)
            v.wait_ge(const_in, 16)
            v.tensor_copy(base[:], const_of("region")).then_inc(setup_dve, 1)
            v.tensor_copy(token_i[:], const_of("token")).then_inc(setup_dve, 1)
            v.tensor_copy(ident16[:], ident).then_inc(setup_dve, 1)
            v.tensor_copy(before16[:], before).then_inc(setup_dve, 1)
            v.wait_ge(setup_pool, 4)
            for c in range(2):
                a0 = CONST["padtoken"][0] + c
                v.tensor_copy(pad[:, c, ROW - 1:ROW].bitcast(I32), consts[:, a0:a0 + 1]).then_inc(setup_dve, 1)

            v.wait_ge(setup_dve, 13)

            def step(n, par):
                def moments():
                    if active(n, 0):
                        plainly(v, (S["stats1_done"], n + 1), (S["ve1_done"], n))
                        for b in range(B):
                            last = v.bn_aggr(moments1[:, b], stats1[:, b])
                        last.then_inc(S["moments1_done"], 1)

                def largest():
                    if active(n, 5):
                        m = n - 5
                        plainly(v, (S["logit_done"], m + 1))
                        for b in range(B):
                            last = v.max(top[:, b], logit[:, b])
                        last.then_inc(S["top_done"], 1)
                    if active(n, 5):
                        m = n - 5
                        reached(v, "top_done", m)
                        v.tensor_tensor(shifted, logit, top[:, :, 0:1].to_broadcast([P, B, E]),
                                        ALU.subtract).then_inc(S["shifted_done"], 1)
                        for b in range(B):
                            last = v.max_index(top_at[:, b], top[:, b], logit[:, b])
                        last.then_inc(S["top_at_done"], 1)

                def choose():
                    if active(n, 5):
                        m = n - 5
                        reached(v, "top_at_done", m)
                        v.tensor_tensor(pick[:], const_of("experts").unsqueeze(1).unsqueeze(1).to_broadcast([P, B, 2, E]),
                                        top_at[:, :, 0:2].unsqueeze(3).to_broadcast([P, B, 2, E]),
                                        ALU.is_equal).then_inc(S["pick_done"], 1)
                    if active(n, 5):
                        m = n - 5
                        reached(v, "pick_done", m)
                        reached(v, "rank_ps", m - 1)
                        v.tensor_tensor(mask[:], pick[:, :, 0], pick[:, :, 1], ALU.add).then_inc(S["mask_done"], 1)

                def place():
                    if active(n, 5):
                        m, mp = n - 5, 1 - par
                        reached(v, "exp_done", m)
                        v.tensor_reduce(esum, shifted, AX.X, ALU.add).then_inc(S["esum_done"], 1)
                        reached(v, "mask_done", m)
                        v.tensor_tensor(masked, shifted, mask[:], ALU.mult).then_inc(S["masked_done"], 1)
                        reached(v, "rank_ps", m)
                        reached(v, "base_done", m - 1)
                        v.tensor_tensor(slots, ps_rank, base[:].unsqueeze(1).to_broadcast([P, B, E]),
                                        ALU.add).then_inc(S["slots_done"], 1)
                        reached(v, "esum_done", m)
                        v.reciprocal(rsum, esum).then_inc(S["rsum_done"], 1)
                        reached(v, "slots_done", m)
                        v.tensor_tensor(base[:], ps_total, base[:], ALU.add).then_inc(S["base_done"], 1)
                        v.tensor_tensor(picked[:], pick[:], slots.unsqueeze(2).to_broadcast([P, B, 2, E]),
                                        ALU.mult).then_inc(S["picked_done"], 1)
                        reached(v, "rsum_done", m)
                        reached(v, "masked_done", m)
                        loaded(v, row_out[mp], m - 2, mp, 64)
                        v.tensor_tensor(row[:, mp, :, D:D + E], masked, rsum.unsqueeze(2).to_broadcast([P, B, E]),
                                        ALU.mult).then_inc(S["gates_done"], 1)
                        reached(v, "picked_done", m)
                        with nc.allow_low_precision(reason="whole numbers below 2**24"):
                            v.tensor_reduce(slot_i[:, mp], picked[:].rearrange("p b k e -> p (b k) e"), AX.X,
                                            ALU.add).then_inc(S["slot_i_done"], 1)

                if is_int(n) and n > NCH + 1:
                    largest()
                    choose()
                if active(n, 0):
                    plainly(v, (x_in[par], (n - par) * 8 + 16))
                    for b in range(B):
                        last = v.bn_stats(stats1[:, b], xt[:, par, b])
                    last.then_inc(S["stats1_done"], 1)
                if is_int(n) and n < 3:
                    moments()
                if active(n, 1):
                    m = n - 1
                    reached(v, "xT_done", m)
                    reached(v, "xcol_done", m - 1)
                    last = v.tensor_tensor(xnT[:, 1, 1 - par, :, :, 0:P].rearrange("p b k t -> p (b k) t"),
                                           ps_xT.rearrange("p b k t -> p (b k) t"),
                                           xnT[:, 0, 1 - par, :, :, 0:P].rearrange("p b k t -> p (b k) t"),
                                           ALU.subtract)
                    if not is_int(m) or m > 0:
                        last = v.tensor_tensor(xnT[:, 1, par, :, :, P:P + 1].rearrange("p b k t -> p (b k) t"),
                                               ps_xT[:, :, :, 0:1].rearrange("p b k t -> p (b k) t"),
                                               xnT[:, 0, par, :, :, P:P + 1].rearrange("p b k t -> p (b k) t"),
                                               ALU.subtract)
                    last.then_inc(S["xlo_done"], 1)
                if is_int(n) and n - 1 == NCH:
                    reached(v, "xcol_done", NCH - 1)
                    v.tensor_copy(xnT[:, 1, par, :, :, P:P + 1].rearrange("p b k t -> p (b k) t"),
                                  zcol[:]).then_inc(S["xlo_done"], 1)
                if active(n, 3):
                    m = n - 3
                    reached(v, "faded_done", m)
                    reached(v, "state_ps", m)
                    reached(v, "read_ps", m)
                    for side in range(2):
                        d = slice(side * HD, (side + 1) * HD)
                        last = v.tensor_tensor(state[d, :, :, d].rearrange("p b k i -> p (b k) i"),
                                               ps_state[d, :, :, d].rearrange("p b k i -> p (b k) i"),
                                               faded[d, :, :, d].rearrange("p b k i -> p (b k) i"), ALU.add)
                    last.then_inc(S["state_done"], 1)
                if not (is_int(n) and n < 3):
                    moments()
                if not is_int(n) or n <= NCH + 1:
                    largest()
                if active(n, 3):
                    m = n - 3
                    reached(v, "proj_ps", m)
                    reached(v, "res_done", m)
                    v.scalar_tensor_tensor(out=res_of(m), in0=ps_proj, scalar=1.0 / WSCALE, in1=res_of(m),
                                           op0=ALU.mult, op1=ALU.add).then_inc(S["x1_done"], 1)
                if active(n, 2):
                    m = n - 2
                    if is_int(m) and m == 0:
                        v.wait_ge(setup_act, 7)
                        v.scalar_tensor_tensor(out=proj16[:, 1].rearrange("p w c -> p (w c)"),
                                               in0=proj_words.rearrange("p w c -> p (w c)"), scalar=WSCALE,
                                               in1=proj16[:, 0].rearrange("p w c -> p (w c)"), op0=ALU.mult,
                                               op1=ALU.subtract).then_inc(setup_dve, 1)
                        for side in range(2):
                            for k in range(KD):
                                v.tensor_tensor(decayM[:, side, k, :], decayM[:, side, k, :], before,
                                                ALU.mult).then_inc(setup_dve, 1)
                        v.wait_ge(setup_dve, 18)
                    reached(v, "score_ps", m)
                    reached(v, "read_ps", m - 1)
                    for b in range(B):
                        last = v.tensor_tensor(scores[:, b].rearrange("p s k t -> p s (k t)"), ps_score[:, :, b],
                                               decayM[:].rearrange("p s k t -> p s (k t)"), ALU.mult)
                    last.then_inc(S["score_done"], 1)
                if active(n, 3):
                    m = n - 3
                    plainly(v, (S["x1_done"], m + 1))
                    for b in range(B):
                        last = v.bn_stats(stats2[:, b], res_of(m)[:, b])
                    last.then_inc(S["stats2_done"], 1)
                if active(n, 1):
                    m = n - 1
                    if is_int(m) and m == 0:
                        v.wait_ge(setup_act, 6)
                    reached(v, "read_ps", m - 2)
                    for b in range(B):
                        last = v.tensor_tensor(queries[:, 1 - par, b, :, 0:P - 1], ps_xT[:, b, :, 1:P],
                                               decayQ[:, :, 0:P - 1], ALU.mult)
                    last.then_inc(S["queries_done"], 1)
                if active(n, 3):
                    m = n - 3
                    plainly(v, (S["stats2_done"], m + 1), (S["ve2_done"], m))
                    for b in range(B):
                        last = v.bn_aggr(moments2[:, b], stats2[:, b])
                    last.then_inc(S["moments2_done"], 1)
                if is_int(n) and n > NCH + 1:
                    place()
                if not is_int(n) or n <= NCH + 1:
                    choose()
                if active(n, 0):
                    reached(v, "rs1_done", n)
                    reached(v, "xT_ps", n - 2)
                    reached(v, "keys_done", n - 2)
                    reached(v, "res_done", n - 2)
                    for b in range(B):
                        last = v.tensor_scalar(xn[:, par, b], xt[:, par, b], moments1[:, b, 0:1], rs1[:, b:b + 1],
                                               ALU.subtract, ALU.mult)
                    last.then_inc(S["xn_done"], 1)
                if active(n, 4):
                    m = n - 4
                    reached(v, "logit_ps", m)
                    reached(v, "top_at_done", m - 1)
                    v.tensor_copy(logit, ps_logit).then_inc(S["logit_done"], 1)
                if active(n, 3):
                    m = n - 3
                    reached(v, "rs2_done", m)
                    reached(v, "mT_ps", m - 2)
                    reached(v, "lo_done", m - 2)
                    for b in range(B):
                        last = v.tensor_scalar(xm[:, 1 - par, b], res_of(m)[:, b], moments2[:, b, 0:1],
                                               rs2[:, b:b + 1], ALU.subtract, ALU.mult)
                    last.then_inc(S["xm_done"], 1)
                if not is_int(n) or n <= NCH + 1:
                    place()
                if is_int(n) and n > NCH and active(n, 4):
                    m = n - 4
                    reached(v, "hi_done", m)
                    words = row[:, par, :, 0:D].bitcast(F16)
                    v.tensor_tensor(words[:, :, D:2 * D], xm[:, par], words[:, :, 0:D],
                                    ALU.subtract).then_inc(S["lo_done"], 1)
                if active(n, 2):
                    m = n - 2
                    reached(v, "read_done", m)
                    for to, frm, slot in ((slice(1, P + 1), slice(0, P), par), (slice(0, 1), slice(P - 1, P), 1 - par)):
                        last = v.tensor_tensor(readsT[:, 1, slot, :, :, to].rearrange("p b k t -> p (b k) t"),
                                               ps_read[:, :, :, frm].rearrange("p b k t -> p (b k) t"),
                                               readsT[:, 0, slot, :, :, to].rearrange("p b k t -> p (b k) t"),
                                               ALU.subtract)
                    last.then_inc(S["readlo_done"], 1)

            stage_one(v, step)

            count = [0]

            def link(ins):
                count[0] += 1
                ins.then_inc(table_step, 1)
                v.wait_ge(table_step, count[0])

            cnt, tiles, ends = (tab[:, i * E:(i + 1) * E] for i in range(3))
            t_exp, t_begin, t_off, t_end, t_own, t_base, t_start, t_shift = (
                tab[:, 3 * E + i * NT:3 * E + (i + 1) * NT] for i in range(8))
            J = TOK // TILE
            tileno = const_of("tile")
            spread = lambda x: x.unsqueeze(1).to_broadcast([P, NT, E])
            reached(v, "base_done", NCH - 1)
            link(v.tensor_tensor(cnt, base[:], const_of("region"), ALU.subtract))
            c3 = cmp[:, 0:E * J].rearrange("p (e j) -> p e j", e=E)
            link(v.tensor_tensor(c3, cnt.unsqueeze(2).to_broadcast([P, E, J]),
                                 const_of("step").unsqueeze(1).to_broadcast([P, E, J]), ALU.is_gt))
            link(v.tensor_reduce(tiles, c3, AX.X, ALU.add))
            c4 = cmp[:, 0:E * E].rearrange("p (e j) -> p e j", e=E)
            link(v.tensor_tensor(c4, tiles.unsqueeze(1).to_broadcast([P, E, E]),
                                 const_of("upto").rearrange("p (e j) -> p e j", e=E), ALU.mult))
            link(v.tensor_reduce(ends, c4, AX.X, ALU.add))
            c5 = cmp[:, 0:NT * E].rearrange("p (t e) -> p t e", e=E)
            c6 = cmp2[:].rearrange("p (t e) -> p t e", e=E)
            link(v.tensor_tensor(c5, tileno.unsqueeze(2).to_broadcast([P, NT, E]), spread(ends), ALU.is_ge))
            v.tensor_reduce(t_exp, c5, AX.X, ALU.add)
            link(v.scalar_tensor_tensor(out=c6, in0=c5, scalar=float(E * CAP), in1=spread(base[:]), op0=ALU.mult,
                                        op1=ALU.add))
            v.tensor_reduce(t_end, c6, AX.X, ALU.min)
            link(v.tensor_tensor(c5, c5, spread(ends), ALU.mult))
            link(v.tensor_reduce(t_begin, c5, AX.X, ALU.max))
            v.tensor_scalar(t_own, t_exp, float(E), None, ALU.is_lt)
            v.tensor_scalar(t_base, t_exp, float(CAP), float(2 * TILE), ALU.mult, ALU.add)
            link(v.tensor_tensor(t_off, tileno, t_begin, ALU.subtract))
            link(v.scalar_tensor_tensor(out=t_base, in0=t_off, scalar=float(TILE), in1=t_base, op0=ALU.mult,
                                        op1=ALU.add))
            link(v.tensor_tensor(t_start, t_base, t_end, ALU.min))
            v.tensor_tensor(t_shift, t_base, t_start, ALU.subtract)
            link(v.scalar_tensor_tensor(out=t_start, in0=t_start, scalar=float(-TILE), in1=t_own, op0=ALU.add,
                                        op1=ALU.mult))
            v.tensor_copy(tile_row_i, t_start)
            link(v.tensor_scalar(t_exp, t_exp, float(E - 1), None, ALU.min))
            link(v.tensor_copy(tile_exp_i, t_exp))
            v.sem_inc(table_done, 1)
            stored(v)
            for s in range(2):
                v.wait_ge(row_out[s], 64 * NCH // 2)
            reached(v, "logit_ps", NCH - 1)
            v.sem_inc(buffers_free, 1)

            def split(i, pair):
                came(v, "act_done", i, 4, pair)
                came(v, "l2_done", i - 1, 4, pair)
                hi = h_hi[:, pair].rearrange("p m t -> p (m t)")
                v.tensor_copy(hi, act[:, pair % 2]).then_inc(S2["hhi_done"], 1)
                came(v, "hhi_done", i, 4, pair)
                v.tensor_tensor(h_lo[:, pair].rearrange("p m t -> p (m t)"), act[:, pair % 2], hi,
                                ALU.subtract).then_inc(S2["split_done"], 1)

            def step2(i, par):
                if has(i + 1):
                    at_i = tile_exp_i[0:1, i + 1:i + 2] if is_int(i) else tile_exp_i[0:1, bass.ds(i + 1, 1)]
                    e = v.value_load(at_i, min_val=0, max_val=E - 1)

                def split_low(part):
                    came(v, "whi_done", i + 1, 4, part)
                    w = 2 * part * PIECE
                    v.scalar_tensor_tensor(out=wcur[:, 1 - par, w + PIECE:w + 2 * PIECE],
                                           in0=weights[:, bass.ds(e * EW + part * PIECE, PIECE)], scalar=WSCALE,
                                           in1=wcur[:, 1 - par, w:w + PIECE], op0=ALU.mult,
                                           op1=ALU.subtract).then_inc(S2["wcur_done"], 1)

                if has(i + 1):
                    split_low(0)
                if has(i):
                    split(i, 0)
                if has(i + 1):
                    split_low(1)
                if has(i):
                    split(i, 1)
                if has(i - 1):
                    for c in range(2):
                        came(v, "l2_done", i - 1, 4)
                        v.wait_ge(b2_in[1 - par], (i - 1 - (1 - par)) * 8 + 16)
                        if not is_int(i) or i >= 3:
                            v.wait_ge(added, (i - 2) * 32)
                        v.scalar_tensor_tensor(out=yout[:, 1 - par, c], in0=ps_y[:, 1 - par, c], scalar=1.0 / WSCALE,
                                               in1=b2_cur[:, 1 - par], op0=ALU.mult,
                                               op1=ALU.add).then_inc(S2["ybias_done"], 1)
                if has(i + 1):
                    split_low(2)
                if has(i):
                    split(i, 2)
                if has(i + 1):
                    v.wait_ge(tile_ld[1 - par], ((i + 1) - (1 - par)) * 8 + 16)
                    came(v, "yout_done", i - 1, 2)
                    came(v, "act_done", i - 1, 4)
                    v.tensor_copy(b1_cur[:, 1 - par], b1T[:].rearrange("p e m -> p (e m)")[:, bass.ds(e * MF, MF)])
                    shift = t_shift[:, i + 1:i + 2] if is_int(i) else t_shift[:, bass.ds(i + 1, 1)]
                    v.scalar_tensor_tensor(out=gate_cur[:, 1 - par], in0=const_of("place"), scalar=shift,
                                           in1=tile_in[:, 1 - par, :, bass.ds(e, 1)].rearrange("p c w -> p (c w)"),
                                           op0=ALU.is_ge, op1=ALU.mult).then_inc(S2["prep_done"], 1)
                    split_low(3)
                if has(i):
                    split(i, 3)

            stage_two(v, step2)

        @block.tensor
        def _(pe):
            pe.wait_ge(const_in, 16)
            three = [(k, x, w) for k in range(KD) for x, w in HIGH_LOW]
            for _ in range(8):
                pe.matmul(ps_state[:, 0, 0], ident, ident, start=True, stop=True)

            def step(n, par):
                if active(n, 1):
                    m = n - 1
                    reached(pe, "xn_done", m)
                    reached(pe, "queries_done", m - 1)
                    for b in range(B):
                        for k in range(KD):
                            last = pe.transpose(ps_xT[:, b, k], xn[:, 1 - par, b, k * P:(k + 1) * P], ident)
                    last.then_inc(S["xT_ps"], 1)
                if active(n, 4):
                    m = n - 4
                    reached(pe, "xm_done", m)
                    reached(pe, "logit_done", m - 1)
                    for b in range(B):
                        for k in range(KD):
                            last = pe.transpose(ps_mT[:, b, k], xm[:, par, b, k * P:(k + 1) * P], ident)
                    last.then_inc(S["mT_ps"], 1)
                if active(n, 3):
                    m, mp = n - 3, 1 - par
                    reached(pe, "readlo_done", m)
                    reached(pe, "x1_done", m - 1)
                    if not is_int(n) or n - 6 >= 0:
                        reached(pe, "base_done", n - 6)
                    for b in range(B):
                        for at, (k, x, w) in enumerate(three):
                            last = pe.matmul(ps_proj[:, b], readsT[:, x, mp, b, k, 0:P], wrT16[:, w, k],
                                             start=(at == 0), stop=(at == len(three) - 1))
                    last.then_inc(S["proj_ps"], 1)
                if active(n, 2):
                    m = n - 2
                    reached(pe, "xlo_done", m + 1)
                    reached(pe, "score_done", m - 1)
                    for b in range(B):
                        for side in range(2):
                            d = slice(side * HD, (side + 1) * HD)
                            for k in range(KD):
                                for at, (x, y) in enumerate(HIGH_LOW):
                                    last = pe.matmul(ps_score[:, side, b, k * P:(k + 1) * P],
                                                     xnT[d, x, par, b, k, 0:P], xnT[d, y, par, b, k, 1:P + 1],
                                                     start=(at == 0), stop=(at == 2))
                    last.then_inc(S["score_ps"], 1)
                    reached(pe, "val_done", m - 1)
                    if is_int(m) and m == 0:
                        pe.wait_ge(setup_dve, 14)
                    for b in range(B):
                        for at, (k, x, w) in enumerate(three):
                            last = pe.matmul(ps_val[:, b], xnT[:, x, par, b, k, 1:P + 1], wwT16[:, w, k],
                                             start=(at == 0), stop=(at == len(three) - 1))
                    last.then_inc(S["val_ps"], 1)
                if active(n, 4):
                    m = n - 4
                    reached(pe, "mT_done", m)
                    if is_int(m) and m == 0:
                        pe.wait_ge(gate_in, 32)
                    for b in range(B):
                        for k in range(KD):
                            last = pe.matmul(ps_logit[:, b], xmT[:, b, k], gateT[:, k], start=(k == 0),
                                             stop=(k == KD - 1))
                    last.then_inc(S["logit_ps"], 1)
                if active(n, 2):
                    m = n - 2
                    reached(pe, "val_done", m)
                    reached(pe, "state_done", m - 1)
                    reached(pe, "queries_done", m)
                    if is_int(m) and m == 0:
                        pe.wait_ge(setup_pool, 2)
                    reached(pe, "score_done", m)
                    reached(pe, "readlo_done", m - 1)
                    for b in range(B):
                        for k in range(KD):
                            pe.matmul(ps_read[:, b, k], state[:, b, k], queries[:, par, b, k], start=True, stop=True)
                            for side in range(2):
                                h = 2 * k + side
                                last = pe.matmul(ps_read[side * HD:(side + 1) * HD, b, k],
                                                 vals[:, b, h * HD:(h + 1) * HD], scores[:, b, side, k],
                                                 start=False, stop=True, skip_group_check=True)
                    last.then_inc(S["read_ps"], 1)
                if active(n, 5):
                    m = n - 5
                    reached(pe, "mask_done", m)
                    if is_int(m) and m == 0:
                        pe.wait_ge(setup_dve, 18)
                    reached(pe, "x1_done", min(n - 3, NCH - 1) if is_int(n) else n - 3)
                    pe.matmul(ps_rank, before16[:], mask[:], start=True, stop=True)
                    pe.matmul(ps_rank[:, 1], ones16[:], mask[:, 0], start=False, stop=True, skip_group_check=True)
                    pe.matmul(ps_total, ones16[:], mask[:, 0], start=True, stop=False)
                    pe.matmul(ps_total, ones16[:], mask[:, 1], start=False, stop=True).then_inc(S["rank_ps"], 1)
                if active(n, 2):
                    m = n - 2
                    reached(pe, "keys_done", m)
                    for b in range(B):
                        for k in range(KD):
                            last = pe.matmul(ps_state[:, b, k], keys[:, par, b, k * P:(k + 1) * P],
                                             vals[:, b, k * P:(k + 1) * P], start=True, stop=True)
                    last.then_inc(S["state_ps"], 1)

            stage_one(pe, step)

            pe.wait_ge(table_done, 1)
            pe.wait_ge(buffers_free, 1)
            for _ in range(8):
                pe.matmul(psum[:, 0, :], ident16[:], proj16[:, 0, 0], start=True, stop=True)
            w1_of = lambda par, k, lo, m: wcur[:, par, k * 2 * PIECE + lo * PIECE + m * P:][:, 0:P]
            w2_of = lambda par, m, lo: wcur[:, par, (2 + m // 4) * 2 * PIECE + lo * PIECE + (m % 4) * D:][:, 0:D]

            def first(i, par, pair):
                s = pair % 2
                if pair == 0:
                    came(pe, "wcur_done", i, 4, 1)
                    pe.wait_ge(tileT_ld[par], (i - par) * 8 + 16)
                if pair >= 2:
                    came(pe, "act_done", i, 4, pair - 2)
                else:
                    came(pe, "act_done", i - 1, 4, pair + 2)
                for mm in range(2):
                    m = 2 * pair + mm
                    n = 0
                    for k in range(KD):
                        for lo, part in ((0, k), (0, KD + k), (1, k)):
                            last = pe.matmul(ps_h[:, s, mm], w1_of(par, k, lo, m), tileT[:, par, part],
                                             start=(n == 0), stop=(n == 3 * KD - 1))
                            n += 1
                last.then_inc(S2["h_ps"], 1)

            def second(i, par, pair):
                s = pair
                came(pe, "split_done", i, 4, pair)
                if pair % 2 == 0:
                    came(pe, "wcur_done", i, 4, 2 + pair // 2)
                if pair == 0:
                    came(pe, "ybias_done", i - 2, 2)
                for mm in range(2):
                    m = 2 * pair + mm
                    for c in range(2):
                        hh = h_hi[:, s, mm, c * P:(c + 1) * P]
                        hl = h_lo[:, s, mm, c * P:(c + 1) * P]
                        for n, (lhs, lo) in enumerate(((hh, 0), (hh, 1), (hl, 0))):
                            last = pe.matmul(ps_y[:, par, c], lhs, w2_of(par, m, lo), start=(m == 0 and n == 0),
                                             stop=(m == MF - 1 and n == 2))
                last.then_inc(S2["l2_done"], 1)

            def step2(i, par):
                if has(i):
                    first(i, par, 0)
                if has(i - 1):
                    second(i - 1, 1 - par, 2)
                if has(i):
                    first(i, par, 1)
                if has(i - 1):
                    second(i - 1, 1 - par, 3)
                if has(i):
                    first(i, par, 2)
                    second(i, par, 0)
                    first(i, par, 3)
                    second(i, par, 1)

            stage_two(pe, step2)


def kernel(L0_attn_out, L0_attn_W_write, L0_attn_W_read, L0_attn_decay, L0_attn_log_alpha,
           L0_ffn_gate_w, L0_ffn_w1, L0_ffn_b1, L0_ffn_w2, L0_ffn_b2):
    import concourse.bacc as bacc
    from concourse.bass_utils import run_bass_kernel_spmd

    blocks = lambda w: np.ascontiguousarray(w.reshape(KD, P, -1).transpose(1, 0, 2))
    w1 = np.asarray(L0_ffn_w1).transpose(1, 2, 0).reshape(E, KD, P, F)
    w2 = np.asarray(L0_ffn_w2).transpose(1, 2, 0).reshape(E, 2, 4, P, D)
    w2 = w2.transpose(0, 1, 3, 2, 4).reshape(E, 2, P, 4 * D)
    arrays = {
        "x": np.ascontiguousarray(L0_attn_out),
        "w_write": blocks(np.asarray(L0_attn_W_write).T),
        "w_read": blocks(np.asarray(L0_attn_W_read).T),
        "decay": np.ascontiguousarray(L0_attn_decay),
        "log_alpha": np.ascontiguousarray(L0_attn_log_alpha),
        "gate_w": blocks(np.asarray(L0_ffn_gate_w).T),
        "experts": np.ascontiguousarray(np.concatenate([w1, w2], axis=1).reshape(NPIECE, P, PIECE)),
        "b1": np.ascontiguousarray(np.asarray(L0_ffn_b1).reshape(E, MF, P).transpose(2, 0, 1)),
        "b2": np.ascontiguousarray(L0_ffn_b2),
        "const": constants(),
    }
    nc = bacc.Bacc("TRN2", target_bir_lowering=False, num_devices=1)
    args = [nc.dram_tensor(f"in_{n}", v.shape, mybir.dt.from_np(v.dtype), kind="ExternalInput").ap()
            for n, v in arrays.items()]
    out = nc.dram_tensor("out", (TOK + TILE, D), F32, kind="ExternalOutput").ap()
    build(nc, *args, out)
    r = run_bass_kernel_spmd(nc, [{f"in_{n}": v for n, v in arrays.items()}], core_ids=[0])
    return np.asarray(r.results[0]["out"])[:TOK].reshape(B, T, D)
```
